# Optimizing a Trainium2 kernel written in Bass

```python
import numpy as np
import jax
import jax.numpy as jnp

def _softmax(x, axis=-1):
    return jax.nn.softmax(x, axis=axis)

def _gelu(x):
    return jax.nn.gelu(x, approximate=True)

def _silu(x):
    return jax.nn.silu(x)

def _sigmoid(x):
    return jax.nn.sigmoid(x)

def _layernorm(x, axis=-1, eps=1e-05):
    m = jnp.mean(x, axis=axis, keepdims=True)
    v = jnp.var(x, axis=axis, keepdims=True)
    return (x - m) / jnp.sqrt(v + eps)

def _scatter_add(tgt, idx, src, axis=0):
    return tgt.at[idx].add(src)

def _segment_sum(src, seg, n):
    return jax.ops.segment_sum(src, seg, n)
kernel_name = 'mk_flamingo_gated_d1_seqx_r8_5a0d71'

def setup_inputs(seed: int=0):
    np.random.seed(seed)
    _w = jnp.asarray

    def _rec_inputs():
        import jax
        import jax.numpy as jnp
        _rk = jax.random.key(seed)
        x = 7.22e-05 + 1 * jax.random.normal(jax.random.fold_in(_rk, 1), (32, 64, 512), jnp.float32)
        _lenS = 64 - jax.random.randint(jax.random.fold_in(_rk, 7), (32,), 0, max(1, 64 // 4) + 1, jnp.int32)
        _lenS2 = 64 - jax.random.randint(jax.random.fold_in(_rk, 8), (32,), 0, max(1, 64 // 4) + 1, jnp.int32)
        _ctx_4096P = jax.random.normal(jax.random.fold_in(_rk, 11), (32, 16, 512), jnp.float32)
        _ctx_4096c = jax.random.dirichlet(jax.random.fold_in(_rk, 511), 0.3 * jnp.ones((16,), jnp.float32), (32, 64))
        _ctx_4096t = jnp.einsum('bsk,bkd->bsd', _ctx_4096c, _ctx_4096P)
        _ctx_4096t = _ctx_4096t * jax.lax.rsqrt(jnp.mean(jnp.square(_ctx_4096t)) + 1e-12) * 0.953939
        ctx_4096 = 4.13588e-05 + 0.999923 * (_ctx_4096t + 0.3 * jax.random.normal(jax.random.fold_in(_rk, 611), (32, 64, 512), jnp.float32))
        _g = jax.random.normal(jax.random.fold_in(_rk, 9001), (2, 1), jnp.float32)
        _g = jnp.sign(_g) * jnp.maximum(jnp.abs(_g), 1.0) + (_g == 0) * 1.0
        g_xattn = _g[0]
        g_ffn = _g[1]
        return (x, ctx_4096, g_xattn, g_ffn)
    x, ctx_4096, g_xattn, g_ffn = _rec_inputs()

    def _L0_xattn_setup():
        import jax, jax.numpy as jnp
        import numpy as np
        HEADS = 8
        WINDOW = 16

        def _pointwise(W, b, t):
            return jnp.einsum('oc,bct->bot', W, t) + b[None, :, None]
        key = jax.random.key(seed)
        ks = jax.random.split(key, 10)
        B, C, T = (4, 64, 512)
        s = 0.02
        return {'x': jax.random.normal(ks[0], (B, C, T), jnp.float32), 'cond': jax.random.normal(ks[1], (B, C, T), jnp.float32), 'Wq': jax.random.normal(ks[2], (C, C), jnp.float32) * s, 'bq': jnp.zeros((C,), jnp.float32), 'Wk': jax.random.normal(ks[3], (C, C), jnp.float32) * s, 'bk': jnp.zeros((C,), jnp.float32), 'Wv': jax.random.normal(ks[4], (C, C), jnp.float32) * s, 'bv': jnp.zeros((C,), jnp.float32), 'Wo': jax.random.normal(ks[5], (C, C), jnp.float32) * s, 'bo': jnp.zeros((C,), jnp.float32)}
    _L0_xattn_all = _L0_xattn_setup()
    _L0_xattn_in = {k: v for k, v in _L0_xattn_all.items() if k in ('Wq', 'bq', 'Wk', 'bk', 'Wv', 'bv', 'Wo', 'bo')}
    del _L0_xattn_all

    def _L0_ffn_setup():
        import jax, jax.numpy as jnp
        import numpy as np
        N_STREAMS = 4
        DIM = 128
        SINKHORN_ITERS = 50
        SINKHORN_TAU = 0.1
        RMS_EPS = 1.1920929e-07

        def sinkhorn_log(logits, num_iters=SINKHORN_ITERS, tau=SINKHORN_TAU):
            Z = logits / tau
            u0 = jnp.zeros(Z.shape[:-1], Z.dtype)
            v0 = jnp.zeros_like(u0)

            def step(carry, _):
                u, v = carry
                u = -jax.nn.logsumexp(Z + v[..., None, :], axis=-1)
                v = -jax.nn.logsumexp(Z + u[..., :, None], axis=-2)
                return ((u, v), None)
            (u, v), _ = jax.lax.scan(step, (u0, v0), None, length=num_iters)
            return jnp.exp(Z + u[..., :, None] + v[..., None, :])
        key = jax.random.key(seed)
        ks = jax.random.split(key, 6)
        B, T = (4, 256)
        n, C = (N_STREAMS, DIM)
        wd = n * C
        x = jax.random.normal(ks[0], (B, T, wd), dtype=jnp.float32)
        W_res = 0.01 * jax.random.normal(ks[1], (n * n, wd), dtype=jnp.float32)
        W_pre = 0.01 * jax.random.normal(ks[2], (n, wd), dtype=jnp.float32)
        W_post = 0.01 * jax.random.normal(ks[3], (n, wd), dtype=jnp.float32)
        H_res_base = jnp.full((n, n), -0.5, dtype=jnp.float32)
        H_res_base = H_res_base.at[jnp.arange(n), jnp.arange(n)].set(0.0)
        H_pre_base = jnp.zeros((n,), dtype=jnp.float32).at[0].set(1.0)
        H_post_base = jnp.zeros((n,), dtype=jnp.float32)
        gate = jnp.array([5.0], dtype=jnp.float32)
        W_branch = 1.0 / np.sqrt(C) * jax.random.normal(ks[4], (C, C), dtype=jnp.float32)
        return {'x': x, 'W_res': W_res, 'W_pre': W_pre, 'W_post': W_post, 'H_res_base': H_res_base, 'H_pre_base': H_pre_base, 'H_post_base': H_post_base, 'gate': gate, 'W_branch': W_branch}
    _L0_ffn_all = _L0_ffn_setup()
    _L0_ffn_in = {k: v for k, v in _L0_ffn_all.items() if k in ('W_res', 'W_pre', 'W_post', 'H_res_base', 'H_pre_base', 'H_post_base', 'gate', 'W_branch')}
    del _L0_ffn_all
    return {'x': x, 'ctx_4096': ctx_4096, 'g_xattn': g_xattn, 'g_ffn': g_ffn, 'L0_xattn_Wq': _L0_xattn_in['Wq'], 'L0_xattn_bq': _L0_xattn_in['bq'], 'L0_xattn_Wk': _L0_xattn_in['Wk'], 'L0_xattn_bk': _L0_xattn_in['bk'], 'L0_xattn_Wv': _L0_xattn_in['Wv'], 'L0_xattn_bv': _L0_xattn_in['bv'], 'L0_xattn_Wo': _L0_xattn_in['Wo'], 'L0_xattn_bo': _L0_xattn_in['bo'], 'L0_ffn_W_res': _L0_ffn_in['W_res'], 'L0_ffn_W_pre': _L0_ffn_in['W_pre'], 'L0_ffn_W_post': _L0_ffn_in['W_post'], 'L0_ffn_H_res_base': _L0_ffn_in['H_res_base'], 'L0_ffn_H_pre_base': _L0_ffn_in['H_pre_base'], 'L0_ffn_H_post_base': _L0_ffn_in['H_post_base'], 'L0_ffn_gate': _L0_ffn_in['gate'], 'L0_ffn_W_branch': _L0_ffn_in['W_branch']}

def reference(x, ctx_4096, g_xattn, g_ffn, L0_xattn_Wq, L0_xattn_bq, L0_xattn_Wk, L0_xattn_bk, L0_xattn_Wv, L0_xattn_bv, L0_xattn_Wo, L0_xattn_bo, L0_ffn_W_res, L0_ffn_W_pre, L0_ffn_W_post, L0_ffn_H_res_base, L0_ffn_H_pre_base, L0_ffn_H_post_base, L0_ffn_gate, L0_ffn_W_branch):
    import jax
    import jax.numpy as jnp

    def _L0_xattn_ref(x, cond, Wq, bq, Wk, bk, Wv, bv, Wo, bo):
        import jax, jax.numpy as jnp
        import numpy as np
        HEADS = 8
        WINDOW = 16

        def _pointwise(W, b, t):
            return jnp.einsum('oc,bct->bot', W, t) + b[None, :, None]
        B, C, T = x.shape
        H, W = (HEADS, WINDOW)
        hd = C // H
        scale = hd ** (-0.5)
        pad_left = W // 2
        pad_right = W - pad_left - 1
        q = _pointwise(Wq, bq, x)
        k = _pointwise(Wk, bk, cond)
        v = _pointwise(Wv, bv, cond)
        k = jnp.pad(k, ((0, 0), (0, 0), (pad_left, pad_right)))
        v = jnp.pad(v, ((0, 0), (0, 0), (pad_left, pad_right)))
        idx = jnp.arange(T)[:, None] + jnp.arange(W)[None, :]
        k_win = k[:, :, idx].reshape(B, H, hd, T, W)
        v_win = v[:, :, idx].reshape(B, H, hd, T, W)
        qh = q.reshape(B, H, hd, T)
        dots = jnp.einsum('bhdt,bhdtw->bhtw', qh, k_win) * scale
        attn = jax.nn.softmax(dots, axis=-1)
        out = jnp.einsum('bhtw,bhdtw->bhdt', attn, v_win)
        out = out.reshape(B, C, T)
        return _pointwise(Wo, bo, out)

    def _L0_ffn_ref(x, W_res, W_pre, W_post, H_res_base, H_pre_base, H_post_base, gate, W_branch):
        import jax, jax.numpy as jnp
        import numpy as np
        N_STREAMS = 4
        DIM = 128
        SINKHORN_ITERS = 50
        SINKHORN_TAU = 0.1
        RMS_EPS = 1.1920929e-07

        def sinkhorn_log(logits, num_iters=SINKHORN_ITERS, tau=SINKHORN_TAU):
            Z = logits / tau
            u0 = jnp.zeros(Z.shape[:-1], Z.dtype)
            v0 = jnp.zeros_like(u0)

            def step(carry, _):
                u, v = carry
                u = -jax.nn.logsumexp(Z + v[..., None, :], axis=-1)
                v = -jax.nn.logsumexp(Z + u[..., :, None], axis=-2)
                return ((u, v), None)
            (u, v), _ = jax.lax.scan(step, (u0, v0), None, length=num_iters)
            return jnp.exp(Z + u[..., :, None] + v[..., None, :])
        B, T, nC = x.shape
        n = N_STREAMS
        C = nC // n
        x_norm = x * jax.lax.rsqrt(jnp.mean(x * x, axis=-1, keepdims=True) + RMS_EPS)
        H_res_logits = (x_norm @ W_res.T).reshape(B, T, n, n) + H_res_base
        H_pre_logits = x_norm @ W_pre.T + H_pre_base
        H_post_logits = x_norm @ W_post.T + H_post_base
        H_res = sinkhorn_log(H_res_logits)
        H_pre = jax.nn.softmax(H_pre_logits, axis=-1)
        H_post = jax.nn.softmax(H_post_logits, axis=-1)
        g = jax.nn.sigmoid(gate)[0]
        I = jnp.eye(n, dtype=H_res.dtype)
        H_res = (1.0 - g) * I + g * H_res
        x_streams = x.reshape(B, T, n, C)
        x_pre = jnp.einsum('btnc,btn->btc', x_streams, H_pre)
        y = x_pre @ W_branch
        x_mixed = jnp.einsum('btij,btjc->btic', H_res, x_streams)
        y_distributed = jnp.einsum('btc,btn->btnc', y, H_post)
        return (x_mixed + y_distributed).reshape(B, T, nC)
    x = x + jnp.tanh(g_xattn[0]) * _L0_xattn_ref(_layernorm(x, axis=-1), ctx_4096, L0_xattn_Wq, L0_xattn_bq, L0_xattn_Wk, L0_xattn_bk, L0_xattn_Wv, L0_xattn_bv, L0_xattn_Wo, L0_xattn_bo)
    x = x + jnp.tanh(g_ffn[0]) * _L0_ffn_ref(_layernorm(x, axis=-1), L0_ffn_W_res, L0_ffn_W_pre, L0_ffn_W_post, L0_ffn_H_res_base, L0_ffn_H_pre_base, L0_ffn_H_post_base, L0_ffn_gate, L0_ffn_W_branch)
    return x

_drawn_inputs = setup_inputs


def setup_inputs(seed=0):
    import zlib

    import numpy as np

    out = dict(_drawn_inputs(seed))
    spreads = {'L0_xattn_bq': (0.0, 0.8),
     'L0_xattn_bk': (0.0, 2.0),
     'L0_xattn_bv': (0.0, 0.642),
     'L0_xattn_bo': (0.0, 0.1),
     'L0_ffn_H_post_base': (0.0, 0.335)}
    factors = {'ctx_4096': 8.0, 'L0_xattn_Wq': 8.0, 'L0_xattn_Wk': 8.0, 'L0_xattn_Wv': 8.0}
    for name, (base, spread) in spreads.items():
        noise = np.random.default_rng([zlib.crc32(name.encode()), seed]).standard_normal(out[name].shape)
        drawn = base * np.exp(spread * noise) if base else spread * noise
        out[name] = jnp.asarray(drawn.astype(out[name].dtype))
    for name, factor in factors.items():
        out[name] = (out[name] * factor).astype(out[name].dtype)
    return out
```

```python
from contextlib import ExitStack

import numpy as np
import concourse.bass as bass
from concourse import mybir

F32 = mybir.dt.float32
BF16 = mybir.dt.bfloat16
ALU = mybir.AluOpType
ACT = mybir.ActivationFunctionType
AX = mybir.AxisListType

P = 128
B, C, T = 32, 64, 512
HEADS, WINDOW = 8, 16
HD = C // HEADS
SCALE = float(HD) ** -0.5
PAD = WINDOW // 2
U, V = 4, 4
TB = 32
NTB = T // TB
KW = 48
NBLK = NTB + 1
TP = NBLK * TB
VW = TB + 1
PAIRS = B // 2
GT = 4
NG = NTB // GT
GROUPS = PAIRS * NG
NS, DIM = 4, 128
NTOK = B * C
TILES = NTOK * NS // P
QT = P // TB
NLOG = NS * NS + 2 * NS
NCO = 2 * NS + 1
ITERS = 50
TAU = 0.1
LN_EPS = 1e-5
RMS_EPS = 1.1920929e-07
NEG = -1e30
LIFT = 2.0 ** 100
LN_LIFT = 100 * float(np.log(2.0))

C_BQ, C_BK, C_BV, C_BO, C_GX, C_GF, C_GATE, C_BASE = 0, 1, 2, 3, 4, 5, 6, 7
NSMALL = C_BASE + NLOG
K_ID, K_MASK, K_TOK, K_HEAD = 0, P, P + KW, 2 * P + KW
NCONST = K_HEAD + V


class Step:

    def __init__(self, i, c):
        self.i, self.c, self.fixed = i, c, isinstance(i, int)

    def at(self, off):
        return Step(self.i, self.c + off)

    def exists(self):
        return not self.fixed or 0 <= self.p < PAIRS

    @property
    def p(self):
        return self.i * 2 + self.c

    @property
    def b(self):
        return self.c % 2

    @property
    def uses(self):
        return self.i + (self.c // 2 + 1)


class Group:

    def __init__(self, step, g):
        self.step, self.g = step.at(g // NG), g % NG

    def at(self, off):
        return Group(self.step, self.g + off)

    def exists(self):
        return self.step.exists()

    @property
    def n(self):
        return self.step.i * (2 * NG) + (self.step.c * NG + self.g)

    @property
    def b(self):
        return self.g % 2


def build(nc, x, ctxin, small, consts, w4, wl, wb, out, xn_dram, co_dram):
    with ExitStack() as ctx:
        def sb(name, shape, dt=F32):
            return ctx.enter_context(nc.sbuf_tensor(name, shape, dt))

        def pb(name, shape):
            return ctx.enter_context(nc.psum_tensor(name, shape, F32))

        def sem(name):
            return ctx.enter_context(nc.semaphore(name))

        def sem2(name):
            return [sem(f"{name}{b}") for b in range(2)]

        small_sb = sb("small_sb", [P, NSMALL])
        consts_sb = sb("consts_sb", [P, NCONST])
        w4_sb = sb("w4_sb", [P, 4, P])
        wl_sb = sb("wl_sb", [P, NS, NLOG])
        wb_sb = sb("wb_sb", [P, DIM])
        ident = consts_sb[:, K_ID:K_ID + P]
        head_mask = consts_sb[:, K_HEAD:K_HEAD + V]
        ident_bf = sb("ident_bf", [P, P], BF16)
        mask_bf = sb("mask_bf", [P, KW], BF16)
        gains = sb("gains", [P, 8])
        bk_head = sb("bk_head", [P, V])
        x_in = [sb(f"x_in{b}", [P, T]) for b in range(2)]
        ctx_in = [sb(f"ctx_in{b}", [P, T]) for b in range(2)]
        x_res = [sb(f"x_res{b}", [P, T]) for b in range(2)]
        xn = [sb(f"xn{b}", [P, T]) for b in range(2)]
        v_sb = [sb(f"v_sb{b}", [P, TP]) for b in range(2)]
        q_bd = [sb(f"q_bd{b}", [P, NTB, U, TB]) for b in range(2)]
        k_bd = [sb(f"k_bd{b}", [P, V, TP]) for b in range(2)]
        v_t = [sb(f"v_t{b}", [P, NBLK, VW]) for b in range(2)]
        v_bd = [sb(f"v_bd{b}", [P, U, NBLK, VW]) for b in range(2)]
        stats1 = sb("stats1", [P, 6])
        mv1 = [sb(f"mv1_{b}", [P, 2]) for b in range(2)]
        ln1 = [sb(f"ln1_{b}", [P, 4]) for b in range(2)]
        negmax = [sb(f"negmax{b}", [P, GT * V]) for b in range(2)]
        nm_hi = [sb(f"nm_hi{b}", [P, GT * V], BF16) for b in range(2)]
        nm_lo = [sb(f"nm_lo{b}", [P, GT * V], BF16) for b in range(2)]
        prob = [sb(f"prob{b}", [P, GT * V, 2 * TB]) for b in range(2)]
        prob_t = [sb(f"prob_t{b}", [P, 2, GT, P]) for b in range(2)]
        den = [sb(f"den{b}", [P, GT, U]) for b in range(2)]
        rden = [sb(f"rden{b}", [P, GT, U]) for b in range(2)]
        o_t = [sb(f"o_t{b}", [P, NTB * U, HD]) for b in range(2)]
        o_c = [sb(f"o_c{b}", [P, T]) for b in range(2)]
        x2 = [sb(f"x2_{b}", [P, T]) for b in range(2)]
        stats2 = sb("stats2", [P, 6])
        mv2 = [sb(f"mv2_{b}", [P, 2]) for b in range(2)]
        ln2 = [sb(f"ln2_{b}", [P, 4]) for b in range(2)]
        xn2 = [sb(f"xn2_{b}", [P, T]) for b in range(2)]
        mv_all = sb("mv_all", [P, PAIRS, 2])
        xr = [sb(f"xr{b}", [P, QT, DIM]) for b in range(2)]
        xr_t = [sb(f"xr_t{b}", [P, QT * P]) for b in range(2)]
        z_all = sb("z_all", [P, PAIRS, QT * DIM])
        logit = sb("logit", [P, PAIRS, NLOG])
        s_ps = [pb(f"s_ps{b}", [P, 2, 512]) for b in range(2)]
        o_ps = pb("o_ps", [P, GT, 256])
        a_ps = pb("a_ps", [P, 512])
        b_ps = pb("b_ps", [P, 512])

        NLOAD = 5
        NZERO = 12

        w_ld, zeroed, vt_zero, const_rdy, gain_rdy, settled = sem("w_ld"), sem("zeroed"), sem("vt_zero"), sem("const_rdy"), sem("gain_rdy"), sem("settled")
        act_g, vec_g = sem("act_g"), sem("vec_g")
        x_ld, c_ld, r_ld, xr_ld = sem2("x_ld"), sem2("c_ld"), sem2("r_ld"), sem2("xr_ld")
        vx, xn_st = sem2("vx"), sem2("xn_st")
        st1_raw, st1, ln1_a, y1, nw1, xn_rdy = (sem(s) for s in ("st1_raw", "st1", "ln1_a", "y1", "nw1", "xn_rdy"))
        q_mm, k_mm, v_mm, q_ev, k_ev, v_ev, vt = (sem(s) for s in ("q_mm", "k_mm", "v_mm", "q_ev", "k_ev", "v_ev", "vt"))
        sc, mx, hi, lo, sub, ex, tr, pv, dn, rd, ov, nrm = (
            sem(s) for s in ("sc", "mx", "hi", "lo", "sub", "ex", "tr", "pv", "dn", "rd", "ov", "nrm"))
        oc, wo, xres, x2_rdy = sem("oc"), sem("wo"), sem("xres"), sem("x2_rdy")
        st2_raw, st2, mvc, ln2_a, y2, nw2, xn2_rdy = (
            sem(s) for s in ("st2_raw", "st2", "mvc", "ln2_a", "y2", "nw2", "xn2_rdy"))
        xt_mm, xt_ev, l_mm, l_ev, z_mm, z_ev = (sem(s) for s in ("xt_mm", "xt_ev", "l_mm", "l_ev", "z_mm", "z_ev"))

        def settle(eng):
            eng.sem_inc(settled, 1)

        def run_pairs(eng, program):
            for i in (-1, 0, 1):
                for c in range(2):
                    program(Step(i, c))
            with eng.Fori(2, PAIRS // 2 - 1) as i:
                for c in range(2):
                    program(Step(i, c))
            for i in (PAIRS // 2 - 1, PAIRS // 2):
                for c in range(2):
                    program(Step(i, c))
            program(Step(PAIRS // 2 + 1, 0))

        def row(t, s):
            return t[:, bass.ds(s.p, 1), :].rearrange("p a n -> p (a n)")

        x_pair = x.rearrange("(q b) c t -> q (b c) t", b=2)
        ctx_pair = ctxin.rearrange("(q b) c t -> q (b c) t", b=2)
        xn_pair = xn_dram.rearrange("(q r) n -> q r n", r=P)
        xn_tile = xn_dram.rearrange("(q t r) (j n) -> q (r j) t n", t=QT, r=TB, j=NS)

        def pick(ap, s):
            return ap[bass.ds(s.p, 1)].rearrange("a r n -> (a r) n")

        def pick_tile(ap, s):
            return ap[bass.ds(s.p, 1)].rearrange("a r t n -> (a r) t n")

        hbd = [sb(f"hbd{b}", [P, QT, TB, NS]) for b in range(2)]
        gbd = [sb(f"gbd{b}", [P, QT, TB, NS]) for b in range(2)]
        out_sb = [sb(f"out_sb{b}", [P, QT, DIM]) for b in range(2)]
        coef = sb("coef", [P, PAIRS, NS, NCO])
        crow = sb("crow", [P, PAIRS, QT * NCO])
        tok = sb("tok", [P, 8, PAIRS])
        gates = sb("gates", [P, PAIRS, 2, NS])
        gates_m = sb("gates_m", [P, 2, PAIRS, 2])
        m4 = sb("m4", [P, PAIRS, NS, NS])
        e4 = sb("e4", [P, PAIRS, NS, NS])
        sums = sb("sums", [P, PAIRS, NS])
        lns = sb("lns", [P, PAIRS, NS])
        recs = sb("recs", [P, PAIRS, NS])
        vec_b, act_b, co_st, cr_ld = sem("vec_b"), sem("act_b"), sem("co_st"), sem("cr_ld")
        red, lnd, rec, mul = sem2("red"), sem2("lnd"), sem2("rec"), sem2("mul")
        xr2_ld, out_st = sem2("xr2_ld"), sem2("out_st")
        h_rdy, g_rdy, mix, out_rdy = sem("h_rdy"), sem("g_rdy"), sem("mix"), sem("out_rdy")

        def stage_a(block):

            @block.sync
            def _(sp):
                sp.dma_start(small_sb[:], small).then_inc(w_ld, 16)
                sp.dma_start(consts_sb[:], consts).then_inc(w_ld, 16)
                sp.dma_start(w4_sb[:], w4).then_inc(w_ld, 16)
                sp.dma_start(wl_sb[:], wl).then_inc(w_ld, 16)
                sp.dma_start(wb_sb[:], wb).then_inc(w_ld, 16)
                sp.wait_ge(zeroed, NZERO)

                def pair(s):
                    s2, s1, m1, m2 = s.at(2), s.at(1), s.at(-1), s.at(-2)
                    if s2.exists():
                        if s.exists():
                            sp.wait_ge(xn_rdy, s.p + 1)
                        sp.dma_start(x_in[s2.b][:], pick(x_pair, s2)).then_inc(x_ld[s2.b], 16)
                        if s.exists():
                            sp.wait_ge(v_mm, s.p + 1)
                            settle(sp)
                        sp.dma_start(ctx_in[s2.b][:], pick(ctx_pair, s2)).then_inc(c_ld[s2.b], 16)
                    if m1.exists():
                        if m1.at(-2).exists():
                            sp.wait_ge(x2_rdy, m1.p - 1)
                        sp.dma_start(x_res[m1.b][:], pick(x_pair, m1)).then_inc(r_ld[m1.b], 16)
                    if m2.exists():
                        sp.wait_ge(xn2_rdy, m2.p + 1)
                        sp.dma_start(pick(xn_pair, m2), xn2[m2.b][:]).then_inc(xn_st[m2.b], 16)
                    if m2.exists():
                        sp.wait_ge(xn_st[m2.b], m2.uses * 16)
                        settle(sp)
                        if m2.at(-2).exists():
                            sp.wait_ge(xt_mm, m2.p - 1)
                        sp.dma_start(xr[m2.b][:], pick_tile(xn_tile, m2)).then_inc(xr_ld[m2.b], 16)
                    if s1.exists():
                        sp.wait_ge(vt, s1.p + 1)
                        settle(sp)
                        last = Group(s1.at(-2), NG - 1)
                        if last.exists():
                            sp.wait_ge(pv, last.n + 1)
                        for u in range(U):
                            r = slice(TB * u, TB * u + TB)
                            sp.dma_start(v_bd[s1.b][r, u, :, :], v_t[s1.b][r, :, :]).then_inc(vx[s1.b], 16)

                run_pairs(sp, pair)

            @block.tensor
            def _(pe):
                pe.wait_ge(w_ld, 16 * NLOAD)
                pe.wait_ge(const_rdy, 2)
                pe.wait_ge(zeroed, NZERO)

                def scores(n):
                    s = n.step
                    if n.g == 0:
                        pe.wait_ge(q_ev, s.p + 1)
                        pe.wait_ge(k_ev, s.p + 1)
                    if n.at(-2).exists():
                        pe.wait_ge(ex, n.n - 1)
                    for h in range(2):
                        bank = s_ps[n.b][:, h, 0:2 * V * KW]
                        pe.matmul(bank, ident_bf[:], mask_bf[:].unsqueeze(1).broadcast_to([P, 2 * V, KW]),
                                  start=True, stop=False, skip_group_check=True)
                        for e in range(2):
                            tb = n.g * GT + 2 * h + e
                            t0 = tb * TB
                            mm = pe.matmul(s_ps[n.b][:, h, e * V * KW:(e + 1) * V * KW],
                                           q_bd[s.b][:, tb].rearrange("p u t -> p (u t)"),
                                           k_bd[s.b][:, :, t0:t0 + KW], start=False, stop=False, skip_group_check=True)
                    mm.then_inc(sc, 1)

                def subtract_max(n):
                    pe.wait_ge(lo, n.n + 1)
                    for h in range(2):
                        for part in (nm_hi, nm_lo):
                            rhs = part[n.b][:, h * 2 * V:(h + 1) * 2 * V].unsqueeze(2).broadcast_to([P, 2 * V, KW])
                            mm = pe.matmul(s_ps[n.b][:, h, 0:2 * V * KW], ident_bf[:], rhs, start=False,
                                           stop=part is nm_lo, skip_group_check=True)
                    mm.then_inc(sub, 1)

                def values(n):
                    s = n.step
                    if n.g == 0:
                        pe.wait_ge(vx[s.b], s.uses * 16 * U)
                    pe.wait_ge(tr, n.n + 1)
                    if n.at(-1).exists():
                        pe.wait_ge(ov, n.n)
                    for e in range(GT):
                        for k in range(2):
                            mm = pe.matmul(o_ps[:, e, 0:U * VW], prob_t[n.b][:, k, e, :],
                                           v_bd[s.b][:, :, n.g * GT + e + k, :], start=(k == 0), stop=(k == 1))
                    mm.then_inc(pv, 1)

                def rows_transposed(m, s1):
                    pe.wait_ge(xr_ld[m.b], m.uses * 16)
                    if s1.exists():
                        pe.wait_ge(v_ev, s1.p + 1)
                    else:
                        pe.wait_ge(z_ev, m.p)
                    for t in range(QT):
                        mm = pe.transpose(a_ps[:, t * P:(t + 1) * P], xr[m.b][:, t, :], ident)
                    mm.then_inc(xt_mm, 1)

                def logits(m):
                    pe.wait_ge(xt_ev, m.p + 1)
                    if m.at(1).exists():
                        pe.wait_ge(x2_rdy, m.p + 2)
                    else:
                        pe.wait_ge(l_ev, m.p)
                    for j in range(NS):
                        mm = pe.matmul(b_ps[:, 0:NLOG], xr_t[m.b][:, j:QT * P:NS], wl_sb[:, j, :],
                                       start=(j == 0), stop=(j == NS - 1))
                    mm.then_inc(l_mm, 1)

                def branch(m, s1):
                    if s1.exists():
                        pe.wait_ge(q_ev, s1.p + 1)
                    for t in range(QT):
                        mm = pe.matmul(a_ps[:, t * DIM:(t + 1) * DIM], xr_t[m.b][:, t * P:(t + 1) * P], wb_sb[:],
                                       start=True, stop=True)
                    mm.then_inc(z_mm, 1)

                def pair(s):
                    s1, m1, m2, m3 = s.at(1), s.at(-1), s.at(-2), s.at(-3)
                    for g in range(NG):
                        n = Group(s, g)
                        if n.exists():
                            scores(n)
                        if g == 3 and m2.exists():
                            rows_transposed(m2, s1)
                        if n.at(-1).exists():
                            subtract_max(n.at(-1))
                        if n.at(-3).exists():
                            values(n.at(-3))
                        if g == 0 and s1.exists():
                            pe.wait_ge(xn_rdy, s1.p + 1)
                            if m3.exists():
                                pe.wait_ge(xt_ev, m3.p + 1)
                            elif s.exists():
                                pe.wait_ge(v_ev, s.p + 1)
                            pe.matmul(a_ps[:], w4_sb[:, 0, :], xn[s1.b][:], start=True, stop=True).then_inc(q_mm, 1)
                        if g == 0 and m3.exists():
                            logits(m3)
                        if g == 1 and s1.exists():
                            pe.wait_ge(c_ld[s1.b], s1.uses * 16)
                            if m3.exists():
                                pe.wait_ge(l_ev, m3.p + 1)
                            elif m2.exists():
                                pe.wait_ge(x2_rdy, m2.p + 1)
                            elif s.exists():
                                pe.wait_ge(k_ev, s.p + 1)
                            pe.matmul(b_ps[:], w4_sb[:, 1, :], ctx_in[s1.b][:], start=True, stop=True).then_inc(k_mm, 1)
                        if g == 1 and m3.exists():
                            branch(m3, s1)
                        if g == 2 and s1.exists():
                            if m3.exists():
                                pe.wait_ge(z_ev, m3.p + 1)
                            else:
                                pe.wait_ge(q_ev, s1.p + 1)
                            pe.matmul(a_ps[:], w4_sb[:, 2, :], ctx_in[s1.b][:], start=True, stop=True).then_inc(v_mm, 1)
                        if g == 3 and m1.exists():
                            pe.wait_ge(oc, m1.p + 1)
                            if s1.exists():
                                pe.wait_ge(k_ev, s1.p + 1)
                            else:
                                pe.wait_ge(l_ev, m3.p + 1)
                            pe.matmul(b_ps[:], w4_sb[:, 3, :], o_c[m1.b][:], start=True, stop=True).then_inc(wo, 1)

                run_pairs(pe, pair)

            @block.vector
            def _(v):
                v.wait_ge(w_ld, 16 * NLOAD)
                v.tensor_copy(ident_bf[:], ident).then_inc(const_rdy, 1)
                v.tensor_copy(mask_bf[:], consts_sb[:, K_MASK:K_MASK + KW]).then_inc(const_rdy, 1)
                for t in v_t:
                    v.memset(t[:], 0.0).then_inc(vt_zero, 1)
                for t in k_bd:
                    v.memset(t[:], 0.0).then_inc(zeroed, 1)
                v.wait_ge(vt_zero, 2)
                for t in v_t:
                    v.memset(t[:, :, TB:VW], 1.0).then_inc(zeroed, 1)
                v.wait_ge(zeroed, NZERO)
                v.wait_ge(act_g, 3)
                v.tensor_scalar(gains[:, 6:7], gains[:, 2:3], 1.0, None, ALU.add).then_inc(vec_g, 1)
                v.wait_ge(vec_g, 1)
                v.reciprocal(gains[:, 7:8], gains[:, 6:7]).then_inc(vec_g, 1)
                v.wait_ge(vec_g, 2)
                v.tensor_tensor(gains[:, 4:5], gains[:, 7:8], gains[:, 1:2], ALU.mult).then_inc(vec_g, 1)
                v.wait_ge(vec_g, 3)
                v.tensor_tensor(gains[:, 5:6], gains[:, 1:2], gains[:, 4:5], ALU.subtract).then_inc(gain_rdy, 1)
                v.tensor_tensor(gains[:, 3:4], gains[:, 0:1], small_sb[:, C_BO:C_BO + 1], ALU.mult).then_inc(gain_rdy, 1)
                v.tensor_tensor(bk_head[:], head_mask, small_sb[:, C_BK:C_BK + 1].broadcast_to([P, V]),
                                ALU.mult).then_inc(gain_rdy, 1)
                v.wait_ge(gain_rdy, 3)

                def pair(s):
                    s2, s1, m1, m2, m3 = s.at(2), s.at(1), s.at(-1), s.at(-2), s.at(-3)
                    for g in range(NG):
                        n = Group(s, g)
                        if g == 0 and m2.exists():
                            v.wait_ge(wo, m2.p + 1)
                            v.wait_ge(xres, m2.p + 1)
                            if m2.at(-2).exists():
                                v.wait_ge(xn2_rdy, m2.p - 1)
                            v.scalar_tensor_tensor(x2[m2.b][:], b_ps[:], gains[:, 0:1], x_res[m2.b][:],
                                                   ALU.mult, ALU.add).then_inc(x2_rdy, 1)
                            v.wait_ge(x2_rdy, m2.p + 1)
                            if m3.exists():
                                v.wait_ge(mvc, m2.p)
                            v.bn_stats(stats2[:], x2[m2.b][:]).then_inc(st2_raw, 1)
                            v.wait_ge(st2_raw, m2.p + 1)
                            settle(v)
                            v.bn_aggr(mv2[m2.b][:], stats2[:]).then_inc(st2, 1)
                            v.wait_ge(st2, m2.p + 1)
                            v.tensor_copy(row(mv_all, m2), mv2[m2.b][:]).then_inc(mvc, 1)
                        if n.at(-2).exists():
                            m = n.at(-2)
                            v.wait_ge(ex, m.n + 1)
                            if m.at(-2).exists():
                                v.wait_ge(pv, m.n - 1)
                            v.transpose(prob_t[m.b][:].rearrange("p k e (a t) -> p k (e a) t", t=TB),
                                        prob[m.b][:].rearrange("p a (k s) -> p k a s", k=2)).then_inc(tr, 1)
                        if n.exists():
                            v.wait_ge(sc, n.n + 1)
                            if n.at(-2).exists():
                                v.wait_ge(lo, n.n - 1)
                            v.tensor_reduce(negmax[n.b][:].rearrange("p (h a) -> p h a", h=2),
                                            s_ps[n.b][:, :, 0:2 * V * KW].rearrange("p h (a k) -> p h a k", k=KW),
                                            AX.X, ALU.max, negate=True).then_inc(mx, 1)
                        if g == 3 and m1.exists():
                            v.wait_ge(nrm, m1.p * NG + NG)
                            if m1.at(-2).exists():
                                v.wait_ge(wo, m1.p - 1)
                            v.transpose(o_c[m1.b][:], o_t[m1.b][:].rearrange("p a d -> p (a d)")).then_inc(oc, 1)
                        if g == 2 and s2.exists():
                            v.wait_ge(x_ld[s2.b], s2.uses * 16)
                            if s.at(1).exists():
                                v.wait_ge(st1, s2.p)
                            v.bn_stats(stats1[:], x_in[s2.b][:]).then_inc(st1_raw, 1)
                            v.wait_ge(st1_raw, s2.p + 1)
                            if s.exists():
                                v.wait_ge(xn_rdy, s.p + 1)
                            settle(v)
                            v.bn_aggr(mv1[s2.b][:], stats1[:]).then_inc(st1, 1)
                        if g == 3 and s1.exists():
                            v.wait_ge(v_ev, s1.p + 1)
                            if m1.exists():
                                v.wait_ge(vx[s1.b], (s1.uses - 1) * 16 * U)
                            v.transpose(v_t[s1.b][:, :, 0:TB], v_sb[s1.b][:].rearrange("p (a t) -> p a t", t=TB))\
                                .then_inc(vt, 1)
                        if n.at(-3).exists():
                            m = n.at(-3)
                            v.wait_ge(dn, m.n + 1)
                            if m.at(-2).exists():
                                v.wait_ge(nrm, m.n - 1)
                            v.reciprocal(rden[m.b][:], den[m.b][:]).then_inc(rd, 1)
                        if g == 0 and m3.exists():
                            v.wait_ge(l_mm, m3.p + 1)
                            v.tensor_copy(row(logit, m3), b_ps[:, 0:NLOG]).then_inc(l_ev, 1)

                run_pairs(v, pair)

            @block.scalar
            def _(a):
                a.wait_ge(w_ld, 16 * NLOAD)
                a.activation(gains[:, 0:1], small_sb[:, C_GX:C_GX + 1], ACT.Tanh).then_inc(act_g, 1)
                a.activation(gains[:, 1:2], small_sb[:, C_GF:C_GF + 1], ACT.Tanh).then_inc(act_g, 1)
                a.preload_act_table_set("natural_log_exp_and_others")
                a.activation(gains[:, 2:3], small_sb[:, C_GATE:C_GATE + 1], ACT.Exp, scale=-1.0).then_inc(act_g, 1)
                a.wait_ge(zeroed, NZERO)
                a.wait_ge(gain_rdy, 3)

                def pair(s):
                    s2, s1, m2, m3 = s.at(2), s.at(1), s.at(-2), s.at(-3)
                    for g in range(NG):
                        n = Group(s, g)
                        if g == 1 and s1.exists():
                            a.wait_ge(q_mm, s1.p + 1)
                            if s1.at(-2).exists():
                                a.wait_ge(sc, s1.at(-1).p * NG)
                            for u in range(U):
                                r = slice(TB * u, TB * u + TB)
                                ins = a.activation(q_bd[s1.b][r, :, u, :],
                                                   a_ps[r, :].rearrange("p (a t) -> p a t", t=TB),
                                                   ACT.Identity, bias=small_sb[r, C_BQ:C_BQ + 1])
                            ins.then_inc(q_ev, 1)
                        if g == 2 and m3.exists():
                            a.wait_ge(z_mm, m3.p + 1)
                            a.copy(row(z_all, m3), a_ps[:]).then_inc(z_ev, 1)
                        if g == 2 and s1.exists():
                            a.wait_ge(k_mm, s1.p + 1)
                            for h in range(V):
                                ins = a.activation(k_bd[s1.b][:, h, PAD:PAD + T], b_ps[:], ACT.Identity,
                                                   scale=head_mask[:, h:h + 1], bias=bk_head[:, h:h + 1])
                            ins.then_inc(k_ev, 1)
                        if g == 3 and s1.exists():
                            a.wait_ge(v_mm, s1.p + 1)
                            if s1.at(-2).exists():
                                a.wait_ge(vt, s1.p - 1)
                            a.activation(v_sb[s1.b][:, PAD:PAD + T], a_ps[:], ACT.Identity,
                                         bias=small_sb[:, C_BV:C_BV + 1]).then_inc(v_ev, 1)
                        if n.at(-1).exists():
                            m = n.at(-1)
                            a.wait_ge(sub, m.n + 1)
                            if m.at(-2).exists():
                                a.wait_ge(tr, m.n - 1)
                            a.activation(prob[m.b][:, :, 0:KW],
                                         s_ps[m.b][:, :, 0:2 * V * KW].rearrange("p h (a k) -> p h a k", k=KW),
                                         ACT.Exp, scale=SCALE).then_inc(ex, 1)
                        if g == 3 and m2.exists():
                            a.wait_ge(xt_mm, m2.p + 1)
                            if m2.at(-2).exists():
                                a.wait_ge(z_mm, m2.p - 1)
                            a.copy(xr_t[m2.b][:], a_ps[:]).then_inc(xt_ev, 1)
                        if g == 0 and m2.exists():
                            a.wait_ge(st2, m2.p + 1)
                            if m2.at(-2).exists():
                                a.wait_ge(xn2_rdy, m2.p - 1)
                            a.activation(ln2[m2.b][:, 0:1], mv2[m2.b][:, 1:2], ACT.Ln, bias=LN_EPS).then_inc(ln2_a, 1)
                            a.wait_ge(ln2_a, m2.p + 1)
                            a.activation(ln2[m2.b][:, 1:2], ln2[m2.b][:, 0:1], ACT.Exp, scale=-0.5).then_inc(y2, 1)
                        if n.at(-3).exists():
                            m = n.at(-3)
                            a.wait_ge(pv, m.n + 1)
                            if m.at(-2).exists():
                                a.wait_ge(rd, m.n - 1)
                            o_all = o_ps[:, :, 0:U * VW].rearrange("p e (u w) -> p e u w", w=VW)
                            a.copy(den[m.b][:], o_all[:, :, :, TB]).then_inc(dn, 1)
                            if m.g == 0 and m.step.at(-2).exists():
                                a.wait_ge(oc, m.step.p - 1)
                            for h in range(V):
                                r = slice(TB * h, TB * h + TB)
                                dst = o_t[m.step.b][r, m.g * GT * U:(m.g + 1) * GT * U, :]
                                ins = a.copy(dst.rearrange("p (e u) d -> p e u d", u=U),
                                             o_all[r, :, :, h * HD:(h + 1) * HD])
                            ins.then_inc(ov, 1)
                        if g == 2 and s2.exists():
                            a.wait_ge(st1, s2.p + 1)
                            if s.exists():
                                a.wait_ge(xn_rdy, s.p + 1)
                            a.activation(ln1[s2.b][:, 0:1], mv1[s2.b][:, 1:2], ACT.Ln, bias=LN_EPS).then_inc(ln1_a, 1)
                            a.wait_ge(ln1_a, s2.p + 1)
                            a.activation(ln1[s2.b][:, 1:2], ln1[s2.b][:, 0:1], ACT.Exp, scale=-0.5).then_inc(y1, 1)

                run_pairs(a, pair)

            @block.gpsimd
            def _(pool):
                for t in q_bd + v_bd + v_sb + prob:
                    pool.memset(t[:], 0.0).then_inc(zeroed, 1)
                pool.wait_ge(gain_rdy, 3)
                pool.wait_ge(zeroed, NZERO)

                def refine_and_apply(s, mv, ln, step, src, dst, done):
                    var, y, t = mv[:, 1:2], ln[:, 1:2], ln[:, 2:3]
                    settle(pool)
                    pool.tensor_scalar(t, var, LN_EPS, y, ALU.add, ALU.mult).then_inc(step, 1)
                    pool.wait_ge(step, s.p * 3 + 1)
                    settle(pool)
                    pool.tensor_scalar(ln[:, 3:4], t, y, -0.5, ALU.mult, ALU.mult).then_inc(step, 1)
                    pool.wait_ge(step, s.p * 3 + 2)
                    settle(pool)
                    pool.tensor_scalar(t, ln[:, 3:4], 1.5, y, ALU.add, ALU.mult).then_inc(step, 1)
                    pool.wait_ge(step, s.p * 3 + 3)
                    settle(pool)
                    pool.tensor_scalar(dst, src, mv[:, 0:1], t, ALU.subtract, ALU.mult).then_inc(done, 1)

                def pair(s):
                    s2, m1, m2 = s.at(2), s.at(-1), s.at(-2)
                    for g in range(NG):
                        n = Group(s, g)
                        if n.exists():
                            pool.wait_ge(mx, n.n + 1)
                            if n.at(-2).exists():
                                pool.wait_ge(sub, n.n - 1)
                            settle(pool)
                            pool.tensor_copy(nm_hi[n.b][:], negmax[n.b][:]).then_inc(hi, 1)
                            pool.wait_ge(hi, n.n + 1)
                            pool.tensor_tensor(nm_lo[n.b][:], negmax[n.b][:], nm_hi[n.b][:],
                                               ALU.subtract).then_inc(lo, 1)
                        if n.at(-3).exists():
                            m = n.at(-3)
                            pool.wait_ge(ov, m.n + 1)
                            pool.wait_ge(rd, m.n + 1)
                            o = o_t[m.step.b][:, m.g * GT * U:(m.g + 1) * GT * U, :]
                            pool.tensor_tensor(o, o, rden[m.b][:].rearrange("p e u -> p (e u)").unsqueeze(2)
                                               .broadcast_to([P, GT * U, HD]), ALU.mult).then_inc(nrm, 1)
                        if g == 0 and m2.exists():
                            pool.wait_ge(y2, m2.p + 1)
                            if m2.at(-2).exists():
                                pool.wait_ge(xn_st[m2.b], (m2.uses - 1) * 16)
                            refine_and_apply(m2, mv2[m2.b], ln2[m2.b], nw2, x2[m2.b][:], xn2[m2.b][:], xn2_rdy)
                        if g == 1 and m1.exists():
                            pool.wait_ge(r_ld[m1.b], m1.uses * 16)
                            settle(pool)
                            pool.tensor_scalar(x_res[m1.b][:], x_res[m1.b][:], gains[:, 3:4], None,
                                               ALU.add).then_inc(xres, 1)
                        if g == 3 and s2.exists():
                            pool.wait_ge(y1, s2.p + 1)
                            if s.exists():
                                pool.wait_ge(q_mm, s.p + 1)
                            refine_and_apply(s2, mv1[s2.b], ln1[s2.b], nw1, x_in[s2.b][:], xn[s2.b][:], xn_rdy)

                run_pairs(pool, pair)


        def stage_b(block):
            def flat(t):
                return t[:].rearrange("p a b -> p (a b)")

            var, mean = mv_all[:, :, 1], mv_all[:, :, 0]

            @block.scalar
            def _(a):
                done = [0]

                def answer(ins):
                    done[0] += 1
                    ins.then_inc(act_b, 1)
                    return done[0]

                def after(n):
                    a.wait_ge(vec_b, n)

                def ln_exp(src, bias):
                    a.wait_ge(act_b, answer(a.activation(tok[:, 0, :], src, ACT.Ln, bias=bias)))
                    answer(a.activation(tok[:, 1, :], tok[:, 0, :], ACT.Exp, scale=-0.5))

                ln_exp(var, LN_EPS)
                after(VB["w"])
                ln_exp(tok[:, 7, :], 0.0)
                after(VB["gates_sub"])
                answer(a.activation(gates[:], gates[:], ACT.Exp))
                after(VB["z_sub"])
                answer(a.activation(e4[:], m4[:], ACT.Exp, scale=1.0 / TAU))
                after(VB["row_sum"])
                answer(a.activation(lns[:], sums[:], ACT.Ln))
                after(VB["col_sub"])
                answer(a.activation(e4[:], m4[:], ACT.Exp))
                after(VB["col_sum"])
                answer(a.activation(lns[:], sums[:], ACT.Ln))
                after(VB["col_ln"])
                answer(a.activation(m4[:], m4[:], ACT.Exp, bias=LN_LIFT))

                with a.Fori(0, ITERS - 1) as it:
                    for half in range(2):
                        for h in range(2):
                            g = slice(h * PAIRS // 2, (h + 1) * PAIRS // 2)
                            a.wait_ge(red[h], it * 2 + (half + 1))
                            a.activation(lns[:, g, :], sums[:, g, :], ACT.Ln, scale=1.0 / LIFT).then_inc(lnd[h], 1)
                            a.wait_ge(lnd[h], it * 2 + (half + 1))
                            a.activation(recs[:, g, :], lns[:, g, :], ACT.Exp, scale=-1.0).then_inc(rec[h], 1)

            @block.vector
            def _(v):
                n = [0]

                def link(ins, name=None):
                    n[0] += 1
                    ins.then_inc(vec_b, 1)
                    v.wait_ge(vec_b, n[0])
                    assert name is None or VB[name] == n[0], (name, n[0])

                def newton(arg, dst):
                    y, t, w = tok[:, 1, :], tok[:, 0, :], tok[:, 2, :]
                    link(v.tensor_tensor(t, arg, y, ALU.mult))
                    link(v.tensor_tensor(w, t, y, ALU.mult))
                    link(v.tensor_scalar(t, w, -0.5, 1.5, ALU.mult, ALU.add))
                    link(v.tensor_tensor(dst, t, y, ALU.mult))

                v.wait_ge(act_b, 2)
                vare, rstd, rrms, std, diag, w = (tok[:, k, :] for k in (2, 3, 4, 5, 6, 7))
                link(v.tensor_scalar(w, var, LN_EPS, None, ALU.add))
                newton(w, rstd)
                link(v.tensor_tensor(std, w, rstd, ALU.mult))
                link(v.tensor_scalar(diag, std, gains[:, 5:6], None, ALU.add))
                link(v.tensor_tensor(tok[:, 0, :], var, rstd, ALU.mult))
                link(v.tensor_tensor(tok[:, 1, :], tok[:, 0, :], rstd, ALU.mult))
                link(v.tensor_scalar(w, tok[:, 1, :], RMS_EPS, None, ALU.add), "w")
                v.wait_ge(act_b, 4)
                newton(w, rrms)
                link(v.tensor_tensor(logit[:], logit[:], rrms.unsqueeze(2).broadcast_to([P, PAIRS, NLOG]), ALU.mult))
                link(v.tensor_tensor(logit[:], logit[:], small_sb[:, C_BASE:C_BASE + NLOG].unsqueeze(1)
                                     .broadcast_to([P, PAIRS, NLOG]), ALU.add))
                gl = logit[:, :, NS * NS:].rearrange("p a (k n) -> p a k n", k=2)
                link(v.tensor_reduce(gates_m[:, 0], gl, AX.X, ALU.max))
                link(v.tensor_tensor(gates[:], gl, gates_m[:, 0].unsqueeze(3).broadcast_to([P, PAIRS, 2, NS]),
                                     ALU.subtract), "gates_sub")
                zl = logit[:, :, 0:NS * NS].rearrange("p a (i j) -> p a i j", i=NS)
                rows = [P, PAIRS, NS, NS]

                def over_j(t):
                    return t[:].unsqueeze(3).broadcast_to(rows)

                def over_i(t):
                    return t[:].unsqueeze(2).broadcast_to(rows)

                def cols(t):
                    return t[:].rearrange("p a i j -> p a j i")

                link(v.tensor_reduce(sums[:], zl, AX.X, ALU.max))
                link(v.tensor_tensor(m4[:], zl, over_j(sums), ALU.subtract), "z_sub")
                v.wait_ge(act_b, 5)
                link(v.tensor_reduce(gates_m[:, 0], gates[:], AX.X, ALU.add))
                link(v.reciprocal(gates_m[:, 1], gates_m[:, 0]))
                link(v.tensor_tensor(gates[:], gates[:], gates_m[:, 1].unsqueeze(3).broadcast_to([P, PAIRS, 2, NS]),
                                     ALU.mult))
                link(v.tensor_scalar(gates[:, :, 1, :], gates[:, :, 1, :], gains[:, 1:2], None, ALU.mult))
                v.wait_ge(act_b, 6)
                link(v.tensor_reduce(sums[:], e4[:], AX.X, ALU.add), "row_sum")
                v.wait_ge(act_b, 7)
                link(v.scalar_tensor_tensor(m4[:].rearrange("p a i j -> p (a i) j"),
                                            m4[:].rearrange("p a i j -> p (a i) j"), 1.0 / TAU,
                                            flat(lns).unsqueeze(2).broadcast_to([P, PAIRS * NS, NS]),
                                            ALU.mult, ALU.subtract))
                link(v.tensor_reduce(sums[:], cols(m4), AX.X, ALU.max))
                link(v.tensor_tensor(m4[:], m4[:], over_i(sums), ALU.subtract), "col_sub")
                v.wait_ge(act_b, 8)
                link(v.tensor_reduce(sums[:], cols(e4), AX.X, ALU.add), "col_sum")
                v.wait_ge(act_b, 9)
                link(v.tensor_tensor(m4[:], m4[:], over_i(lns), ALU.subtract), "col_ln")
                v.wait_ge(act_b, 10)

                halves = [slice(h * PAIRS // 2, (h + 1) * PAIRS // 2) for h in range(2)]
                half_rows = [P, PAIRS // 2, NS, NS]

                def row_sum(g):
                    return v.tensor_reduce(sums[:, g, :], m4[:, g], AX.X, ALU.add)

                def col_sum(g):
                    return v.tensor_reduce(sums[:, g, :], m4[:, g].rearrange("p a i j -> p a j i"), AX.X, ALU.add)

                for h in range(2):
                    row_sum(halves[h]).then_inc(red[h], 1)
                with v.Fori(0, ITERS - 1) as it:
                    for h in range(2):
                        g = halves[h]
                        v.wait_ge(rec[h], it * 2 + 1)
                        v.tensor_tensor(m4[:, g], m4[:, g], recs[:, g, :].unsqueeze(3).broadcast_to(half_rows),
                                        ALU.mult).then_inc(mul[h], 1)
                        v.wait_ge(mul[h], it * 2 + 1)
                        col_sum(g).then_inc(red[h], 1)
                    for h in range(2):
                        g = halves[h]
                        v.wait_ge(rec[h], it * 2 + 2)
                        v.tensor_tensor(m4[:, g], m4[:, g], recs[:, g, :].unsqueeze(2).broadcast_to(half_rows),
                                        ALU.mult).then_inc(mul[h], 1)
                        v.wait_ge(mul[h], it * 2 + 2)
                        row_sum(g).then_inc(red[h], 1)

                link(v.tensor_scalar(coef[:, :, :, 0:NS], cols(m4), 1.0 / LIFT, gains[:, 4:5], ALU.mult, ALU.mult))
                dg = coef[:].rearrange("p a j k -> p a (j k)")[:, :, 0:NS * NCO:NCO + 1]
                link(v.tensor_tensor(dg, dg, diag.unsqueeze(2).broadcast_to([P, PAIRS, NS]), ALU.add))
                link(v.tensor_tensor(coef[:, :, :, NS:2 * NS], gates[:, :, 0, :].unsqueeze(3).broadcast_to(rows),
                                     gates[:, :, 1, :].unsqueeze(2).broadcast_to(rows), ALU.mult))
                link(v.tensor_copy(coef[:, :, :, 2 * NS], mean.unsqueeze(2).broadcast_to([P, PAIRS, NS])), "coef")

            @block.sync
            def _(sp):
                sp.wait_ge(vec_b, VB["coef"])
                sp.dma_start(co_dram.rearrange("(a p j) k -> p a (j k)", p=P, j=NS),
                             coef[:].rearrange("p a j k -> p a (j k)")).then_inc(co_st, 16)
                sp.wait_ge(co_st, 16)
                sp.dma_start(crow[:].rearrange("p a (t k) -> p (a t) k", k=NCO),
                             co_dram.rearrange("(t p) k -> p t k", p=P)).then_inc(cr_ld, 16)
                sp.wait_ge(cr_ld, 16)

        def stage_c(block):
            out_tile = out.rearrange("(q e) (t c) (j n) -> q e t c j n", e=2, t=2, j=NS)
            out_rows = out.rearrange("b c n -> (b c) n").rearrange("(q t r) (j n) -> q (r j) t n", t=QT, r=TB, j=NS)
            m_ps = [s_ps[b][:, 0, :] for b in range(2)]

            def run_all(eng, program):
                for c in range(2):
                    program(Step(0, c))
                with eng.Fori(1, PAIRS // 2) as i:
                    for c in range(2):
                        program(Step(i, c))

            @block.sync
            def _(sp):
                def pair(s):
                    if s.at(-2).exists():
                        sp.wait_ge(mix, s.p - 1)
                    sp.dma_start(xr[s.b][:], pick_tile(xn_tile, s)).then_inc(xr2_ld[s.b], 16)

                run_all(sp, pair)
                sp.wait_ge(out_st[0], 16 * PAIRS // 2)
                sp.wait_ge(out_st[1], 16 * PAIRS // 2)

            @block.scalar
            def _(a):
                def pair(s):
                    a.wait_ge(out_rdy, s.p + 1)
                    a.dma_start(pick_tile(out_rows, s), out_sb[s.b][:]).then_inc(out_st[s.b], 16)

                run_all(a, pair)

            tok_mask = consts_sb[:, K_TOK:K_TOK + P].rearrange("p (t i) -> p t i", i=NS).unsqueeze(1)\
                .broadcast_to([P, QT, TB, NS])

            def coef_row(s, k):
                return row(crow, s).rearrange("p (t k) -> p t k", k=NCO)[:, :, k:k + NS].unsqueeze(2)\
                    .broadcast_to([P, QT, TB, NS])

            @block.vector
            def _(v):
                def mean_add(s):
                    v.wait_ge(mix, s.p + 1)
                    if s.at(-2).exists():
                        v.wait_ge(out_st[s.b], (s.uses - 1) * 16)
                    mean = row(crow, s).rearrange("p (t k) -> p t k", k=NCO)[:, :, 2 * NS:NCO]
                    v.tensor_tensor(out_sb[s.b][:], m_ps[s.b].rearrange("p (t n) -> p t n", t=QT),
                                    mean.broadcast_to([P, QT, DIM]), ALU.add).then_inc(out_rdy, 1)

                def pair(s):
                    if s.at(-2).exists():
                        v.wait_ge(mix, s.p - 1)
                    v.tensor_tensor(hbd[s.b][:], tok_mask, coef_row(s, 0), ALU.mult).then_inc(h_rdy, 1)
                    if s.at(-1).exists():
                        mean_add(s.at(-1))

                run_all(v, pair)
                mean_add(Step(PAIRS // 2 - 1, 1))

            @block.gpsimd
            def _(pool):
                def pair(s):
                    if s.at(-2).exists():
                        pool.wait_ge(mix, s.p - 1)
                    pool.tensor_tensor(gbd[s.b][:], tok_mask, coef_row(s, NS), ALU.mult).then_inc(g_rdy, 1)

                run_all(pool, pair)

            @block.tensor
            def _(pe):
                def pair(s):
                    pe.wait_ge(xr2_ld[s.b], s.uses * 16)
                    pe.wait_ge(h_rdy, s.p + 1)
                    pe.wait_ge(g_rdy, s.p + 1)
                    if s.at(-2).exists():
                        pe.wait_ge(out_rdy, s.p - 1)
                    for t in range(QT):
                        dst = m_ps[s.b][:, t * DIM:(t + 1) * DIM]
                        pe.matmul(dst, hbd[s.b][:, t].rearrange("p a i -> p (a i)"), xr[s.b][:, t, :],
                                  start=True, stop=False)
                        mm = pe.matmul(dst, gbd[s.b][:, t].rearrange("p a i -> p (a i)"),
                                       row(z_all, s)[:, t * DIM:(t + 1) * DIM], start=False, stop=True)
                    mm.then_inc(mix, 1)

                run_all(pe, pair)

        for stage in (stage_a, stage_b, stage_c):
            with nc.Block() as block:
                stage(block)


VB = {"w": 10, "gates_sub": 18, "z_sub": 20, "row_sum": 25, "col_sub": 28, "col_sum": 29, "col_ln": 30, "coef": 34}


def kernel(**inputs):
    import concourse.bacc as bacc
    from concourse.bass_utils import run_bass_kernel_spmd

    a = {k: np.asarray(val) for k, val in inputs.items()}
    f32 = np.float32

    small = np.zeros((P, NSMALL), f32)
    for col, name in ((C_BQ, "bq"), (C_BK, "bk"), (C_BV, "bv"), (C_BO, "bo")):
        for b in range(2):
            small[b * C:(b + 1) * C, col] = a["L0_xattn_" + name]
    small[:, C_GX], small[:, C_GF], small[:, C_GATE] = a["g_xattn"][0], a["g_ffn"][0], a["L0_ffn_gate"][0]
    small[:, C_BASE:C_BASE + NS * NS] = a["L0_ffn_H_res_base"].reshape(1, -1)
    small[:, C_BASE + NS * NS:C_BASE + NS * NS + NS] = a["L0_ffn_H_pre_base"][None]
    small[:, C_BASE + NS * NS + NS:] = a["L0_ffn_H_post_base"][None]

    consts = np.zeros((P, NCONST), f32)
    for p in range(P):
        consts[p, K_ID + p] = 1.0
        t = p % TB
        consts[p, K_MASK:K_MASK + KW] = NEG
        consts[p, K_MASK + t:K_MASK + t + WINDOW] = 0.0
        consts[p, K_HEAD + (p // HD) % V] = 1.0
        consts[p, K_TOK + (p // NS) * NS:K_TOK + (p // NS) * NS + NS] = 1.0

    w4 = np.zeros((P, 4, P), f32)
    for b in range(2):
        r = slice(b * C, (b + 1) * C)
        for k, name in enumerate(("Wq", "Wk", "Wv")):
            w4[r, k, r] = a["L0_xattn_" + name].T
        for h in range(HEADS):
            to = (h % V) * U * HD + (b * (HEADS // V) + h // V) * HD
            w4[to:to + HD, 3, r] = a["L0_xattn_Wo"].T[h * HD:(h + 1) * HD]

    wl = np.concatenate([a["L0_ffn_W_res"], a["L0_ffn_W_pre"], a["L0_ffn_W_post"]])
    wl = np.ascontiguousarray(wl.reshape(NLOG, NS, DIM).transpose(2, 1, 0))

    arrays = {"x": a["x"], "ctx": a["ctx_4096"], "small": small, "consts": consts, "w4": w4, "wl": wl,
              "wb": a["L0_ffn_W_branch"]}
    nc = bacc.Bacc("TRN2", target_bir_lowering=False, num_devices=1)
    aps = [nc.dram_tensor(k, val.shape, F32, kind="ExternalInput").ap() for k, val in arrays.items()]
    out = nc.dram_tensor("out", (B, C, T), F32, kind="ExternalOutput").ap()
    xn_dram = nc.dram_tensor("xn_scratch", (NTOK, T), F32, kind="Internal").ap()
    co_dram = nc.dram_tensor("coef_scratch", (NTOK * NS, NCO), F32, kind="Internal").ap()
    build(nc, *aps, out, xn_dram, co_dram)
    r = run_bass_kernel_spmd(nc, [{k: np.ascontiguousarray(val) for k, val in arrays.items()}], core_ids=[0])
    return r.results[0]["out"]
```

```python
from contextlib import ExitStack

import numpy as np
import concourse.bass as bass
from concourse import mybir

F32 = mybir.dt.float32
BF16 = mybir.dt.bfloat16
ALU = mybir.AluOpType
ACT = mybir.ActivationFunctionType
AX = mybir.AxisListType

P = 128
B, C, T = 32, 64, 512
HEADS, WINDOW = 8, 16
HD = C // HEADS
SCALE = float(HD) ** -0.5
PAD = WINDOW // 2
U, V = 4, 4
TB = 32
NTB = T // TB
KW = 48
NBLK = NTB + 1
TP = NBLK * TB
VW = TB + 1
PAIRS = B // 2
GT = 4
NG = NTB // GT
GROUPS = PAIRS * NG
NS, DIM = 4, 128
NTOK = B * C
TILES = NTOK * NS // P
QT = P // TB
NLOG = NS * NS + 2 * NS
NG1 = NS + 1
ITERS = 50
TAU = 0.1
LN_EPS = 1e-5
RMS_EPS = 1.1920929e-07
NEG = -1e30
LIFT = 2.0 ** 100
LN_LIFT = 100 * float(np.log(2.0))

C_BQ, C_BK, C_BV, C_BO, C_GX, C_GF, C_GATE, C_BASE = 0, 1, 2, 3, 4, 5, 6, 7
NSMALL = C_BASE + NLOG
K_ID, K_MASK, K_TOK, K_HEAD = 0, P, P + KW, 2 * P + KW
NCONST = K_HEAD + V
NPICK = NS * P + 2 * (NS - 1)


HALVES = 2 * (ITERS - 1)
STREAMS = 3
UNROLL = 7
assert (ITERS - 1) % UNROLL == 0


class Step:

    def __init__(self, i, c, per=2):
        self.i, self.c, self.per, self.fixed = i, c, per, isinstance(i, int)

    def at(self, off):
        return Step(self.i, self.c + off, self.per)

    def exists(self):
        return not self.fixed or 0 <= self.p < PAIRS

    @property
    def p(self):
        return self.i * self.per + self.c

    @property
    def b(self):
        return self.c % 2

    @property
    def uses(self):
        return self.i * (self.per // 2) + (self.c // 2 + 1)


class Group:

    def __init__(self, step, g):
        self.step, self.g = step.at(g // NG), g % NG

    def at(self, off):
        return Group(self.step, self.g + off)

    def exists(self):
        return self.step.exists()

    @property
    def n(self):
        return self.step.i * (2 * NG) + (self.step.c * NG + self.g)

    @property
    def b(self):
        return self.g % 2


def build(nc, x, ctxin, small, consts, pick_rows, w4, wl, wb, out, xn_dram):
    with ExitStack() as ctx:
        def sb(name, shape, dt=F32):
            return ctx.enter_context(nc.sbuf_tensor(name, shape, dt))

        def pb(name, shape):
            return ctx.enter_context(nc.psum_tensor(name, shape, F32))

        def sem(name):
            return ctx.enter_context(nc.semaphore(name))

        def sem2(name):
            return [sem(f"{name}{b}") for b in range(2)]

        small_sb = sb("small_sb", [P, NSMALL])
        consts_sb = sb("consts_sb", [P, NCONST])
        pick_sb = sb("pick_sb", [P, NPICK])
        w4_sb = sb("w4_sb", [P, 4, P])
        wl_sb = sb("wl_sb", [P, NS, NLOG])
        wb_sb = sb("wb_sb", [P, DIM])
        ident = consts_sb[:, K_ID:K_ID + P]
        head_mask = consts_sb[:, K_HEAD:K_HEAD + V]
        ident_bf = sb("ident_bf", [P, P], BF16)
        mask_bf = sb("mask_bf", [P, KW], BF16)
        gains = sb("gains", [P, 8])
        bk_head = sb("bk_head", [P, V])
        x_in = [sb(f"x_in{b}", [P, T]) for b in range(2)]
        ctx_in = [sb(f"ctx_in{b}", [P, T]) for b in range(2)]
        x_res = [sb(f"x_res{b}", [P, T]) for b in range(2)]
        xn = [sb(f"xn{b}", [P, T]) for b in range(2)]
        v_sb = [sb(f"v_sb{b}", [P, TP]) for b in range(2)]
        q_bd = [sb(f"q_bd{b}", [P, NTB, U, TB]) for b in range(2)]
        k_bd = [sb(f"k_bd{b}", [P, V, TP]) for b in range(2)]
        v_t = [sb(f"v_t{b}", [P, NBLK, VW]) for b in range(2)]
        v_bd = [sb(f"v_bd{b}", [P, U, NBLK, VW]) for b in range(2)]
        stats1 = sb("stats1", [P, 6])
        mv1 = [sb(f"mv1_{b}", [P, 2]) for b in range(2)]
        ln1 = [sb(f"ln1_{b}", [P, 4]) for b in range(2)]
        negmax = [sb(f"negmax{b}", [P, GT * V]) for b in range(2)]
        nm_hi = [sb(f"nm_hi{b}", [P, GT * V], BF16) for b in range(2)]
        nm_lo = [sb(f"nm_lo{b}", [P, GT * V], BF16) for b in range(2)]
        prob = [sb(f"prob{b}", [P, GT * V, 2 * TB]) for b in range(2)]
        prob_t = [sb(f"prob_t{b}", [P, 2, GT, P]) for b in range(2)]
        den = [sb(f"den{b}", [P, GT, U]) for b in range(2)]
        rden = [sb(f"rden{b}", [P, GT, U]) for b in range(2)]
        o_t = [sb(f"o_t{b}", [P, NTB * U, HD]) for b in range(2)]
        o_c = [sb(f"o_c{b}", [P, T]) for b in range(2)]
        x2 = [sb(f"x2_{b}", [P, T]) for b in range(2)]
        stats2 = sb("stats2", [P, 6])
        mv2 = [sb(f"mv2_{b}", [P, 2]) for b in range(2)]
        ln2 = [sb(f"ln2_{b}", [P, 4]) for b in range(2)]
        xn2 = [sb(f"xn2_{b}", [P, T]) for b in range(2)]
        mv_all = sb("mv_all", [P, PAIRS, 2])
        xr = [sb(f"xr{b}", [P, QT, DIM]) for b in range(2)]
        xr_all = sb("xr_all", [P, PAIRS, QT * DIM])
        xr_t = [sb(f"xr_t{b}", [P, QT * P]) for b in range(2)]
        z_all = sb("z_all", [P, PAIRS, QT * DIM])
        logit = sb("logit", [P, PAIRS, NLOG])
        s_ps = [pb(f"s_ps{b}", [P, 2, 512]) for b in range(2)]
        o_ps = pb("o_ps", [P, GT, 256])
        a_ps = pb("a_ps", [P, 512])
        b_ps = pb("b_ps", [P, 512])

        NZERO = 13

        small_ld, w_ld, const_ld, wf_ld = (sem(s) for s in ("small_ld", "w_ld", "const_ld", "wf_ld"))
        zeroed, cleared, const_rdy, gain_rdy, settled = (
            sem(s) for s in ("zeroed", "cleared", "const_rdy", "gain_rdy", "settled"))
        act_g, vec_g = sem("act_g"), sem("vec_g")
        x_ld, c_ld, r_ld, xr_ld = sem2("x_ld"), sem2("c_ld"), sem2("r_ld"), sem2("xr_ld")
        vx, xn_st = sem2("vx"), sem2("xn_st")
        st1_raw, st1, ln1_a, y1, nw1, xn_rdy = (sem(s) for s in ("st1_raw", "st1", "ln1_a", "y1", "nw1", "xn_rdy"))
        q_mm, k_mm, v_mm, q_ev, k_ev, v_ev, vt = (sem(s) for s in ("q_mm", "k_mm", "v_mm", "q_ev", "k_ev", "v_ev", "vt"))
        sc, mx, hi, lo, sub, ex, tr, pv, dn, rd, ov, nrm = (
            sem(s) for s in ("sc", "mx", "hi", "lo", "sub", "ex", "tr", "pv", "dn", "rd", "ov", "nrm"))
        oc, wo, xres, x2_rdy = sem("oc"), sem("wo"), sem("xres"), sem("x2_rdy")
        st2_raw, st2, mvc, ln2_a, y2, nw2, xn2_rdy = (
            sem(s) for s in ("st2_raw", "st2", "mvc", "ln2_a", "y2", "nw2", "xn2_rdy"))
        xt_mm, xt_ev, l_mm, l_ev, z_mm, z_ev = (sem(s) for s in ("xt_mm", "xt_ev", "l_mm", "l_ev", "z_mm", "z_ev"))

        def settle(eng):
            eng.sem_inc(settled, 1)

        def run_pairs(eng, program, after_first=lambda: None, before_last=lambda: None):
            program(Step(-1, 0))
            after_first()
            program(Step(-1, 1))
            for i in (0, 1):
                for c in range(2):
                    program(Step(i, c))
            with eng.Fori(2, PAIRS // 2 - 1) as i:
                for c in range(2):
                    program(Step(i, c))
            for i in (PAIRS // 2 - 1, PAIRS // 2):
                for c in range(2):
                    program(Step(i, c))
            before_last()
            program(Step(PAIRS // 2 + 1, 0))

        def row(t, s):
            return t[:, bass.ds(s.p, 1), :].rearrange("p a n -> p (a n)")

        x_pair = x.rearrange("(q b) c t -> q (b c) t", b=2)
        ctx_pair = ctxin.rearrange("(q b) c t -> q (b c) t", b=2)
        xn_pair = xn_dram.rearrange("(q r) n -> q r n", r=P)
        xn_tile = xn_dram.rearrange("(q t r) (j n) -> q (r j) t n", t=QT, r=TB, j=NS)

        def pick(ap, s):
            return ap[bass.ds(s.p, 1)].rearrange("a r n -> (a r) n")

        def pick_tile(ap, s):
            return ap[bass.ds(s.p, 1)].rearrange("a r t n -> (a r) t n")

        hbd = [sb(f"hbd{b}", [P, QT, TB, NS]) for b in range(2)]
        gbd = [sb(f"gbd{b}", [P, QT, TB, NS]) for b in range(2)]
        h_tok = sb("h_tok", [P, PAIRS, NS, NS])
        g_tok = sb("g_tok", [P, PAIRS, NS, NG1])
        h_row = sb("h_row", [P, QT, PAIRS, NS])
        g_row = sb("g_row", [P, QT, PAIRS, NG1])
        tok = sb("tok", [P, 8, PAIRS])
        gates = sb("gates", [P, PAIRS, 2, NS])
        gates_m = sb("gates_m", [P, 2, PAIRS, 2])
        m4 = sb("m4", [P, PAIRS, NS, NS])
        e4 = sb("e4", [P, PAIRS, NS, NS])
        sums = sb("sums", [P, PAIRS, NS])
        lns = sb("lns", [P, PAIRS, NS])
        recs = sb("recs", [P, PAIRS, NS])
        vec_b, act_b = sem("vec_b"), sem("act_b")
        pick_ld, g_mv, g_row_rdy, h_mv, h_row_rdy = (sem(s) for s in ("pick_ld", "g_mv", "g_row_rdy", "h_mv", "h_row_rdy"))
        red, lnd, rec, mul = ([sem(f"{s}{k}") for k in range(STREAMS)] for s in ("red", "lnd", "rec", "mul"))
        xr_all_ld, out_st = sem("xr_all_ld"), sem("out_st")
        g_rdy, gz_mm, gz_ev, y_rdy = sem("g_rdy"), sem("gz_mm"), sem("gz_ev"), sem("y_rdy")
        h_rdy, hx_mm, out_rdy = sem2("h_rdy"), sem("hx_mm"), sem("out_rdy")

        cuts = [PAIRS * k // STREAMS for k in range(STREAMS + 1)]
        streams = [slice(cuts[k], cuts[k + 1]) for k in range(STREAMS)]
        whole = slice(0, PAIRS)

        def over_j(t, g):
            return t[:, g].unsqueeze(3).broadcast_to([P, g.stop - g.start, NS, NS])

        def over_i(t, g):
            return t[:, g].unsqueeze(2).broadcast_to([P, g.stop - g.start, NS, NS])

        def cols(t, g):
            return t[:, g].rearrange("p a i j -> p a j i")

        def flat(t):
            return t[:].rearrange("p a b -> p (a b)") if len(t.shape) == 3 else t[:].rearrange("p a b c -> p (a b c)")

        out_rows = out.rearrange("b c n -> (b c) n").rearrange("(q t r) (j n) -> q (r j) t n", t=QT, r=TB, j=NS)
        m_ps = [s_ps[0][:, 0, :], s_ps[1][:, 0, :], s_ps[0][:, 1, :], s_ps[1][:, 1, :]]
        h_bd = hbd + gbd
        tok_mask = consts_sb[:, K_TOK:K_TOK + P].rearrange("p (t i) -> p t i", i=NS).unsqueeze(1)\
            .broadcast_to([P, QT, TB, NS])

        def run_mix(eng, program, per=2):
            for c in range(per):
                program(Step(0, c, per))
            with eng.Fori(1, PAIRS // per) as i:
                for c in range(per):
                    program(Step(i, c, per))

        def of_pair(t, s, cols):
            return t[:, :, bass.ds(s.p, 1), cols].rearrange("p t a k -> p t (a k)")

        def own_token(t, s):
            return of_pair(t, s, slice(0, NS)).unsqueeze(2).broadcast_to([P, QT, TB, NS])

        def tiles(t):
            return t.rearrange("p (t n) -> p t n", t=QT)

        with nc.Block() as block:

            @block.sync
            def _(sp):
                def load_x(s):
                    sp.dma_start(x_in[s.b][:], pick(x_pair, s)).then_inc(x_ld[s.b], 16)

                def load_ctx(s):
                    sp.dma_start(ctx_in[s.b][:], pick(ctx_pair, s)).then_inc(c_ld[s.b], 16)

                load_x(Step(0, 0))
                sp.dma_start(small_sb[:], small).then_inc(small_ld, 16)
                sp.dma_start(w4_sb[:], w4).then_inc(w_ld, 16)
                load_ctx(Step(0, 0))
                sp.dma_start(consts_sb[:], consts).then_inc(const_ld, 16)
                load_x(Step(0, 1))
                load_ctx(Step(0, 1))
                sp.dma_start(wl_sb[:], wl).then_inc(wf_ld, 16)
                sp.dma_start(wb_sb[:], wb).then_inc(wf_ld, 16)
                sp.dma_start(pick_sb[:], pick_rows).then_inc(pick_ld, 16)

                def pair(s):
                    s2, s1, m1, m2 = s.at(2), s.at(1), s.at(-1), s.at(-2)
                    if s2.exists() and s.exists():
                        sp.wait_ge(xn_rdy, s.p + 1)
                        load_x(s2)
                        sp.wait_ge(v_mm, s.p + 1)
                        settle(sp)
                        load_ctx(s2)
                    if m1.exists():
                        if m1.at(-2).exists():
                            sp.wait_ge(x2_rdy, m1.p - 1)
                        sp.dma_start(x_res[m1.b][:], pick(x_pair, m1)).then_inc(r_ld[m1.b], 16)
                    if m2.exists():
                        sp.wait_ge(xn2_rdy, m2.p + 1)
                        sp.dma_start(pick(xn_pair, m2), xn2[m2.b][:]).then_inc(xn_st[m2.b], 16)
                    if m2.exists():
                        sp.wait_ge(xn_st[m2.b], m2.uses * 16)
                        settle(sp)
                        if m2.at(-2).exists():
                            sp.wait_ge(xt_mm, m2.p - 1)
                        sp.dma_start(xr[m2.b][:], pick_tile(xn_tile, m2)).then_inc(xr_ld[m2.b], 16)
                    if s1.exists():
                        sp.wait_ge(vt, s1.p + 1)
                        settle(sp)
                        last = Group(s1.at(-2), NG - 1)
                        if s1.fixed and s1.p == 0:
                            sp.wait_ge(cleared, 3)
                        if last.exists():
                            sp.wait_ge(pv, last.n + 1)
                        for u in range(U):
                            r = slice(TB * u, TB * u + TB)
                            sp.dma_start(v_bd[s1.b][r, u, :, :], v_t[s1.b][r, :, :]).then_inc(vx[s1.b], 16)

                run_pairs(sp, pair)

                for k in range(4):
                    q = slice(k * PAIRS // 4, (k + 1) * PAIRS // 4)
                    sp.dma_start(xr_all[:, q].rearrange("p q (t n) -> p q t n", t=QT),
                                 xn_tile[q].rearrange("q p t n -> p q t n")).then_inc(xr_all_ld, 16)

                def store(s):
                    sp.wait_ge(out_rdy, s.p + 1)
                    settle(sp)
                    sp.dma_start(pick_tile(out_rows, s), tiles(row(z_all, s))).then_inc(out_st, 16)

                run_mix(sp, store)
                sp.wait_ge(out_st, 16 * PAIRS)

            @block.tensor
            def _(pe):
                pe.wait_ge(w_ld, 16)

                def scores(n):
                    s = n.step
                    if n.g == 0 and s.fixed and s.p == 0:
                        pe.wait_ge(const_rdy, 2)
                        pe.wait_ge(zeroed, NZERO)
                        pe.wait_ge(const_ld, 16)
                    if n.g == 0:
                        pe.wait_ge(q_ev, s.p + 1)
                        pe.wait_ge(k_ev, s.p + 1)
                    if n.at(-2).exists():
                        pe.wait_ge(ex, n.n - 1)
                    for h in range(2):
                        bank = s_ps[n.b][:, h, 0:2 * V * KW]
                        pe.matmul(bank, ident_bf[:], mask_bf[:].unsqueeze(1).broadcast_to([P, 2 * V, KW]),
                                  start=True, stop=False, skip_group_check=True)
                        for e in range(2):
                            tb = n.g * GT + 2 * h + e
                            t0 = tb * TB
                            mm = pe.matmul(s_ps[n.b][:, h, e * V * KW:(e + 1) * V * KW],
                                           q_bd[s.b][:, tb].rearrange("p u t -> p (u t)"),
                                           k_bd[s.b][:, :, t0:t0 + KW], start=False, stop=False, skip_group_check=True)
                    mm.then_inc(sc, 1)

                def subtract_max(n):
                    pe.wait_ge(lo, n.n + 1)
                    for h in range(2):
                        for part in (nm_hi, nm_lo):
                            rhs = part[n.b][:, h * 2 * V:(h + 1) * 2 * V].unsqueeze(2).broadcast_to([P, 2 * V, KW])
                            mm = pe.matmul(s_ps[n.b][:, h, 0:2 * V * KW], ident_bf[:], rhs, start=False,
                                           stop=part is nm_lo, skip_group_check=True)
                    mm.then_inc(sub, 1)

                def values(n):
                    s = n.step
                    if n.g == 0:
                        pe.wait_ge(vx[s.b], s.uses * 16 * U)
                    pe.wait_ge(tr, n.n + 1)
                    if n.at(-1).exists():
                        pe.wait_ge(ov, n.n)
                    for e in range(GT):
                        for k in range(2):
                            mm = pe.matmul(o_ps[:, e, 0:U * VW], prob_t[n.b][:, k, e, :],
                                           v_bd[s.b][:, :, n.g * GT + e + k, :], start=(k == 0), stop=(k == 1))
                    mm.then_inc(pv, 1)

                def rows_transposed(m, s1):
                    pe.wait_ge(xr_ld[m.b], m.uses * 16)
                    if s1.exists():
                        pe.wait_ge(v_ev, s1.p + 1)
                    else:
                        pe.wait_ge(z_ev, m.p)
                    for t in range(QT):
                        mm = pe.transpose(a_ps[:, t * P:(t + 1) * P], xr[m.b][:, t, :], ident)
                    mm.then_inc(xt_mm, 1)

                def logits(m):
                    if m.fixed and m.p == 0:
                        pe.wait_ge(wf_ld, 32)
                    pe.wait_ge(xt_ev, m.p + 1)
                    if m.at(1).exists():
                        pe.wait_ge(x2_rdy, m.p + 2)
                    else:
                        pe.wait_ge(l_ev, m.p)
                    for j in range(NS):
                        mm = pe.matmul(b_ps[:, 0:NLOG], xr_t[m.b][:, j:QT * P:NS], wl_sb[:, j, :],
                                       start=(j == 0), stop=(j == NS - 1))
                    mm.then_inc(l_mm, 1)

                def branch(m, s1):
                    if s1.exists():
                        pe.wait_ge(q_ev, s1.p + 1)
                    for t in range(QT):
                        mm = pe.matmul(a_ps[:, t * DIM:(t + 1) * DIM], xr_t[m.b][:, t * P:(t + 1) * P], wb_sb[:],
                                       start=True, stop=True)
                    mm.then_inc(z_mm, 1)

                def pair(s):
                    s1, m1, m2, m3 = s.at(1), s.at(-1), s.at(-2), s.at(-3)
                    for g in range(NG):
                        n = Group(s, g)
                        if n.exists():
                            scores(n)
                        if g == 3 and m2.exists():
                            rows_transposed(m2, s1)
                        if n.at(-1).exists():
                            subtract_max(n.at(-1))
                        if n.at(-3).exists():
                            values(n.at(-3))
                        if g == 0 and s1.exists():
                            pe.wait_ge(xn_rdy, s1.p + 1)
                            if m3.exists():
                                pe.wait_ge(xt_ev, m3.p + 1)
                            elif s.exists():
                                pe.wait_ge(v_ev, s.p + 1)
                            pe.matmul(a_ps[:], w4_sb[:, 0, :], xn[s1.b][:], start=True, stop=True).then_inc(q_mm, 1)
                        if g == 0 and m3.exists():
                            logits(m3)
                        if g == 1 and s1.exists():
                            pe.wait_ge(c_ld[s1.b], s1.uses * 16)
                            if m3.exists():
                                pe.wait_ge(l_ev, m3.p + 1)
                            elif m2.exists():
                                pe.wait_ge(x2_rdy, m2.p + 1)
                            elif s.exists():
                                pe.wait_ge(k_ev, s.p + 1)
                            pe.matmul(b_ps[:], w4_sb[:, 1, :], ctx_in[s1.b][:], start=True, stop=True).then_inc(k_mm, 1)
                        if g == 1 and m3.exists():
                            branch(m3, s1)
                        if g == 2 and s1.exists():
                            if m3.exists():
                                pe.wait_ge(z_ev, m3.p + 1)
                            else:
                                pe.wait_ge(q_ev, s1.p + 1)
                            pe.matmul(a_ps[:], w4_sb[:, 2, :], ctx_in[s1.b][:], start=True, stop=True).then_inc(v_mm, 1)
                        if g == 3 and m1.exists():
                            pe.wait_ge(oc, m1.p + 1)
                            if s1.exists():
                                pe.wait_ge(k_ev, s1.p + 1)
                            else:
                                pe.wait_ge(l_ev, m3.p + 1)
                            pe.matmul(b_ps[:], w4_sb[:, 3, :], o_c[m1.b][:], start=True, stop=True).then_inc(wo, 1)

                run_pairs(pe, pair)
                pe.wait_ge(ex, GROUPS)
                pe.wait_ge(z_ev, PAIRS)

                def to_rows(src, n, dst, done):
                    for t in range(QT):
                        for j in range(NS):
                            c0 = t * P + NS - 1 - j
                            mm = pe.matmul(dst[:, t * PAIRS * n:(t + 1) * PAIRS * n].rearrange("p (a k) -> p a k", k=n),
                                           pick_sb[:, c0:c0 + P], src[:, :, j, :], start=(j == 0), stop=(j == NS - 1))
                    mm.then_inc(done, 1)

                def branch_mixed(s):
                    pe.wait_ge(g_rdy, s.p + 1)
                    if s.at(-2).exists():
                        pe.wait_ge(gz_ev, s.p - 1)
                    for t in range(QT):
                        mm = pe.matmul(m_ps[s.b][:, t * DIM:(t + 1) * DIM], gbd[s.b][:, t].rearrange("p a i -> p (a i)"),
                                       row(z_all, s)[:, t * DIM:(t + 1) * DIM], start=True, stop=True)
                    mm.then_inc(gz_mm, 1)

                def rows_mixed(s):
                    pe.wait_ge(h_rdy[s.b], s.uses)
                    if s.at(-4).exists():
                        pe.wait_ge(out_rdy, s.p - 3)
                    for t in range(QT):
                        mm = pe.matmul(m_ps[s.c % 4][:, t * DIM:(t + 1) * DIM],
                                       h_bd[s.c % 4][:, t].rearrange("p a i -> p (a i)"),
                                       row(xr_all, s)[:, t * DIM:(t + 1) * DIM], start=True, stop=True)
                    mm.then_inc(hx_mm, 1)

                pe.wait_ge(pick_ld, 16)
                pe.wait_ge(vec_b, VB["g"])
                to_rows(g_tok, NG1, a_ps, g_mv)
                run_mix(pe, branch_mixed)
                pe.wait_ge(vec_b, VB["h"])
                to_rows(h_tok, NS, b_ps, h_mv)
                pe.wait_ge(gz_ev, PAIRS)
                pe.wait_ge(xr_all_ld, 16 * 4)
                run_mix(pe, rows_mixed, 4)

            @block.vector
            def _(v):
                for t in k_bd:
                    v.memset(t[:, :, 0:PAD], 0.0).then_inc(zeroed, 1)
                    v.memset(t[:, :, PAD + T:TP], 0.0).then_inc(zeroed, 1)
                for t in v_sb:
                    v.memset(t[:, 0:PAD], 0.0).then_inc(zeroed, 1)
                    v.memset(t[:, PAD + T:TP], 0.0).then_inc(zeroed, 1)
                for t in v_t:
                    v.memset(t[:, :, TB:VW], 1.0).then_inc(zeroed, 1)
                for t in prob:
                    v.memset(t[:, :, KW:2 * TB], 0.0).then_inc(zeroed, 1)

                def refine_and_apply(s, mv, ln, step, src, dst, done):
                    var, y, t = mv[:, 1:2], ln[:, 1:2], ln[:, 2:3]
                    v.tensor_scalar(t, var, LN_EPS, y, ALU.add, ALU.mult).then_inc(step, 1)
                    v.wait_ge(step, s.p * 3 + 1)
                    v.tensor_scalar(ln[:, 3:4], t, y, -0.5, ALU.mult, ALU.mult).then_inc(step, 1)
                    v.wait_ge(step, s.p * 3 + 2)
                    v.tensor_scalar(t, ln[:, 3:4], 1.5, y, ALU.add, ALU.mult).then_inc(step, 1)
                    v.wait_ge(step, s.p * 3 + 3)
                    v.tensor_scalar(dst, src, mv[:, 0:1], t, ALU.subtract, ALU.mult).then_inc(done, 1)

                def clear():
                    v.wait_ge(const_ld, 16)
                    v.tensor_copy(ident_bf[:], ident).then_inc(const_rdy, 1)
                    v.tensor_copy(mask_bf[:], consts_sb[:, K_MASK:K_MASK + KW]).then_inc(const_rdy, 1)
                    v.wait_ge(act_g, 3)
                    v.tensor_scalar(gains[:, 6:7], gains[:, 2:3], 1.0, None, ALU.add).then_inc(vec_g, 1)
                    v.wait_ge(vec_g, 1)
                    v.reciprocal(gains[:, 7:8], gains[:, 6:7]).then_inc(vec_g, 1)
                    v.wait_ge(vec_g, 2)
                    v.tensor_tensor(gains[:, 4:5], gains[:, 7:8], gains[:, 1:2], ALU.mult).then_inc(vec_g, 1)
                    v.wait_ge(vec_g, 3)
                    v.tensor_tensor(gains[:, 5:6], gains[:, 1:2], gains[:, 4:5], ALU.subtract).then_inc(gain_rdy, 1)
                    v.wait_ge(small_ld, 16)
                    v.tensor_tensor(gains[:, 3:4], gains[:, 0:1], small_sb[:, C_BO:C_BO + 1],
                                    ALU.mult).then_inc(gain_rdy, 1)
                    v.tensor_tensor(bk_head[:], head_mask, small_sb[:, C_BK:C_BK + 1].broadcast_to([P, V]),
                                    ALU.mult).then_inc(gain_rdy, 1)
                    v.wait_ge(gain_rdy, 3)
                    v.wait_ge(zeroed, NZERO)
                    for t in (v_bd[0], q_bd[1], v_bd[1]):
                        v.memset(t[:], 0.0).then_inc(cleared, 1)

                def pair(s):
                    s2, s1, m1, m2, m3 = s.at(2), s.at(1), s.at(-1), s.at(-2), s.at(-3)
                    for g in range(NG):
                        n = Group(s, g)
                        if g == 0 and m2.exists():
                            v.wait_ge(wo, m2.p + 1)
                            v.wait_ge(xres, m2.p + 1)
                            if m2.at(-2).exists():
                                v.wait_ge(xn2_rdy, m2.p - 1)
                            v.scalar_tensor_tensor(x2[m2.b][:], b_ps[:], gains[:, 0:1], x_res[m2.b][:],
                                                   ALU.mult, ALU.add).then_inc(x2_rdy, 1)
                            v.wait_ge(x2_rdy, m2.p + 1)
                            if m3.exists():
                                v.wait_ge(mvc, m2.p)
                            v.bn_stats(stats2[:], x2[m2.b][:]).then_inc(st2_raw, 1)
                            v.wait_ge(st2_raw, m2.p + 1)
                            settle(v)
                            v.bn_aggr(mv2[m2.b][:], stats2[:]).then_inc(st2, 1)
                            v.wait_ge(st2, m2.p + 1)
                            v.tensor_copy(row(mv_all, m2), mv2[m2.b][:]).then_inc(mvc, 1)
                        if g == 1 and m2.exists():
                            v.wait_ge(y2, m2.p + 1)
                            if m2.at(-2).exists():
                                v.wait_ge(xn_st[m2.b], (m2.uses - 1) * 16)
                            refine_and_apply(m2, mv2[m2.b], ln2[m2.b], nw2, x2[m2.b][:], xn2[m2.b][:], xn2_rdy)
                        if g == 3 and s2.exists():
                            v.wait_ge(y1, s2.p + 1)
                            if s.exists():
                                v.wait_ge(q_mm, s.p + 1)
                            refine_and_apply(s2, mv1[s2.b], ln1[s2.b], nw1, x_in[s2.b][:], xn[s2.b][:], xn_rdy)
                        if n.at(-2).exists():
                            m = n.at(-2)
                            v.wait_ge(ex, m.n + 1)
                            if m.at(-2).exists():
                                v.wait_ge(pv, m.n - 1)
                            v.transpose(prob_t[m.b][:].rearrange("p k e (a t) -> p k (e a) t", t=TB),
                                        prob[m.b][:].rearrange("p a (k s) -> p k a s", k=2)).then_inc(tr, 1)
                        if n.exists():
                            v.wait_ge(sc, n.n + 1)
                            if n.at(-2).exists():
                                v.wait_ge(lo, n.n - 1)
                            v.tensor_reduce(negmax[n.b][:].rearrange("p (h a) -> p h a", h=2),
                                            s_ps[n.b][:, :, 0:2 * V * KW].rearrange("p h (a k) -> p h a k", k=KW),
                                            AX.X, ALU.max, negate=True).then_inc(mx, 1)
                        if g == 3 and m1.exists():
                            v.wait_ge(nrm, m1.p * NG + NG)
                            if m1.at(-2).exists():
                                v.wait_ge(wo, m1.p - 1)
                            v.transpose(o_c[m1.b][:], o_t[m1.b][:].rearrange("p a d -> p (a d)")).then_inc(oc, 1)
                        if g == 2 and s2.exists():
                            v.wait_ge(x_ld[s2.b], s2.uses * 16)
                            if s.at(1).exists():
                                v.wait_ge(st1, s2.p)
                            v.bn_stats(stats1[:], x_in[s2.b][:]).then_inc(st1_raw, 1)
                            v.wait_ge(st1_raw, s2.p + 1)
                            if s.exists():
                                v.wait_ge(xn_rdy, s.p + 1)
                            settle(v)
                            v.bn_aggr(mv1[s2.b][:], stats1[:]).then_inc(st1, 1)
                        if g == 3 and s1.exists():
                            v.wait_ge(v_ev, s1.p + 1)
                            if m1.exists():
                                v.wait_ge(vx[s1.b], (s1.uses - 1) * 16 * U)
                            v.transpose(v_t[s1.b][:, :, 0:TB], v_sb[s1.b][:].rearrange("p (a t) -> p a t", t=TB))\
                                .then_inc(vt, 1)
                        if n.at(-3).exists():
                            m = n.at(-3)
                            v.wait_ge(dn, m.n + 1)
                            if m.at(-2).exists():
                                v.wait_ge(nrm, m.n - 1)
                            v.reciprocal(rden[m.b][:], den[m.b][:]).then_inc(rd, 1)
                        if g == 0 and m3.exists():
                            v.wait_ge(l_mm, m3.p + 1)
                            v.tensor_copy(row(logit, m3), b_ps[:, 0:NLOG]).then_inc(l_ev, 1)

                n = [0]

                def link(ins, name=None):
                    n[0] += 1
                    ins.then_inc(vec_b, 1)
                    v.wait_ge(vec_b, n[0])
                    assert name is None or VB[name] == n[0], (name, n[0])

                def newton(arg, dst):
                    y, t, w = tok[:, 1, :], tok[:, 0, :], tok[:, 2, :]
                    link(v.tensor_tensor(t, arg, y, ALU.mult))
                    link(v.tensor_tensor(w, t, y, ALU.mult))
                    link(v.tensor_scalar(t, w, -0.5, 1.5, ALU.mult, ALU.add))
                    link(v.tensor_tensor(dst, t, y, ALU.mult))

                rstd, rrms, std, diag, w = (tok[:, k, :] for k in (3, 4, 5, 6, 7))
                var, mean = mv_all[:, :, 1], mv_all[:, :, 0]

                def deviations():
                    v.wait_ge(act_b, 2)
                    link(v.tensor_scalar(w, var, LN_EPS, None, ALU.add))
                    newton(w, rstd)
                    link(v.tensor_tensor(std, w, rstd, ALU.mult))
                    link(v.tensor_scalar(diag, std, gains[:, 5:6], None, ALU.add))
                    link(v.tensor_tensor(tok[:, 0, :], var, rstd, ALU.mult))
                    link(v.tensor_tensor(tok[:, 1, :], tok[:, 0, :], rstd, ALU.mult))
                    link(v.tensor_scalar(w, tok[:, 1, :], RMS_EPS, None, ALU.add), "w")
                    v.wait_ge(act_b, 4)
                    newton(w, rrms)

                run_pairs(v, pair, clear, deviations)
                v.wait_ge(l_ev, PAIRS)
                link(v.tensor_tensor(logit[:], logit[:], rrms.unsqueeze(2).broadcast_to([P, PAIRS, NLOG]), ALU.mult))
                link(v.tensor_tensor(logit[:], logit[:], small_sb[:, C_BASE:C_BASE + NLOG].unsqueeze(1)
                                     .broadcast_to([P, PAIRS, NLOG]), ALU.add))
                zl = logit[:, :, 0:NS * NS].rearrange("p a (i j) -> p a i j", i=NS)
                link(v.tensor_reduce(sums[:], zl, AX.X, ALU.max))
                link(v.tensor_tensor(m4[:], zl, over_j(sums, whole), ALU.subtract), "z_sub")
                gl = logit[:, :, NS * NS:].rearrange("p a (k n) -> p a k n", k=2)
                gate_shape = [P, PAIRS, 2, NS]
                link(v.tensor_reduce(gates_m[:, 0], gl, AX.X, ALU.max))
                link(v.tensor_tensor(gates[:], gl, gates_m[:, 0].unsqueeze(3).broadcast_to(gate_shape), ALU.subtract),
                     "gates_sub")
                v.wait_ge(act_b, 5)
                link(v.tensor_reduce(sums[:], e4[:], AX.X, ALU.add), "row_sum")
                v.wait_ge(act_b, 7)
                m_rows = m4[:].rearrange("p a i j -> p (a i) j")
                link(v.scalar_tensor_tensor(m_rows, m_rows, 1.0 / TAU,
                                            flat(lns).unsqueeze(2).broadcast_to([P, PAIRS * NS, NS]),
                                            ALU.mult, ALU.subtract))
                link(v.tensor_reduce(sums[:], cols(m4, whole), AX.X, ALU.max))
                link(v.tensor_tensor(m4[:], m4[:], over_i(sums, whole), ALU.subtract), "col_sub")
                link(v.tensor_reduce(gates_m[:, 0], gates[:], AX.X, ALU.add))
                link(v.reciprocal(gates_m[:, 1], gates_m[:, 0]))
                v.wait_ge(act_b, 8)
                link(v.tensor_reduce(sums[:], cols(e4, whole), AX.X, ALU.add), "col_sum")
                link(v.tensor_tensor(gates[:], gates[:], gates_m[:, 1].unsqueeze(3).broadcast_to(gate_shape), ALU.mult))
                link(v.tensor_scalar(gates[:, :, 1, :], gates[:, :, 1, :], gains[:, 1:2], None, ALU.mult))
                v.wait_ge(act_b, 9)
                link(v.tensor_tensor(m4[:], m4[:], over_i(lns, whole), ALU.subtract), "col_ln")
                shape = [P, PAIRS, NS, NS]
                link(v.tensor_tensor(g_tok[:, :, :, 0:NS], gates[:, :, 0, :].unsqueeze(3).broadcast_to(shape),
                                     gates[:, :, 1, :].unsqueeze(2).broadcast_to(shape), ALU.mult))
                link(v.tensor_copy(g_tok[:, :, :, NS], mean.unsqueeze(2).broadcast_to([P, PAIRS, NS])), "g")
                v.wait_ge(act_b, 10)

                def sum_rows(k):
                    v.tensor_reduce(sums[:, streams[k]], m4[:, streams[k]], AX.X, ALU.add).then_inc(red[k], 1)

                def sum_cols(k):
                    v.tensor_reduce(sums[:, streams[k]], cols(m4, streams[k]), AX.X, ALU.add).then_inc(red[k], 1)

                def scale(k, n, over):
                    g = streams[k]
                    v.wait_ge(rec[k], n + 1)
                    v.tensor_tensor(m4[:, g], m4[:, g], over(recs, g), ALU.mult).then_inc(mul[k], 1)

                for k in range(STREAMS):
                    sum_rows(k)
                with v.Fori(0, (ITERS - 1) // UNROLL) as i:
                    for it in range(UNROLL):
                        for half, over, sum_other in ((0, over_j, sum_cols), (1, over_i, sum_rows)):
                            n = i * (2 * UNROLL) + (it * 2 + half)
                            scale(0, n, over)
                            scale(1, n, over)
                            v.wait_ge(mul[0], n + 1)
                            sum_other(0)
                            v.wait_ge(mul[1], n + 1)
                            sum_other(1)
                            scale(2, n, over)
                            v.wait_ge(mul[2], n + 1)
                            sum_other(2)

                v.wait_ge(mul[STREAMS - 1], HALVES)
                done = [VB["g"]]

                def last(ins):
                    done[0] += 1
                    ins.then_inc(vec_b, 1)
                    v.wait_ge(vec_b, done[0])

                last(v.tensor_scalar(h_tok[:], cols(m4, whole), 1.0 / LIFT, gains[:, 4:5], ALU.mult, ALU.mult))
                dg = h_tok[:].rearrange("p a j k -> p a (j k)")[:, :, 0:NS * NS:NS + 1]
                last(v.tensor_tensor(dg, dg, diag.unsqueeze(2).broadcast_to([P, PAIRS, NS]), ALU.add))
                assert done[0] == VB["h"]
                v.wait_ge(h_row_rdy, 1)
                v.wait_ge(gz_mm, PAIRS)

                def rows_out(s):
                    v.wait_ge(hx_mm, s.p + 1)
                    v.wait_ge(y_rdy, s.p + 1)
                    v.tensor_tensor(row(z_all, s), m_ps[s.c % 4], row(z_all, s), ALU.add).then_inc(out_rdy, 1)

                def mix_pair(s):
                    if s.b == 0:
                        if s.at(-4).exists():
                            v.wait_ge(hx_mm, s.p - 3)
                        v.tensor_tensor(h_bd[s.c % 4][:], tok_mask, own_token(h_row, s), ALU.mult).then_inc(h_rdy[0], 1)
                    if s.at(-3).exists():
                        rows_out(s.at(-3))

                run_mix(v, mix_pair, 4)
                for c in range(1, 4):
                    rows_out(Step(PAIRS // 4 - 1, c, 4))

            @block.scalar
            def _(a):
                a.wait_ge(small_ld, 16)
                a.activation(gains[:, 0:1], small_sb[:, C_GX:C_GX + 1], ACT.Tanh).then_inc(act_g, 1)
                a.activation(gains[:, 1:2], small_sb[:, C_GF:C_GF + 1], ACT.Tanh).then_inc(act_g, 1)
                a.preload_act_table_set("natural_log_exp_and_others")
                a.activation(gains[:, 2:3], small_sb[:, C_GATE:C_GATE + 1], ACT.Exp, scale=-1.0).then_inc(act_g, 1)

                def pair(s):
                    s2, s1, m2, m3 = s.at(2), s.at(1), s.at(-2), s.at(-3)
                    for g in range(NG):
                        n = Group(s, g)
                        if g == 1 and s1.exists():
                            a.wait_ge(q_mm, s1.p + 1)
                            if s1.fixed and s1.p < 2:
                                a.wait_ge(cleared if s1.p else zeroed, 3 if s1.p else NZERO)
                            if s1.at(-2).exists():
                                a.wait_ge(sc, s1.at(-1).p * NG)
                            for u in range(U):
                                r = slice(TB * u, TB * u + TB)
                                ins = a.activation(q_bd[s1.b][r, :, u, :],
                                                   a_ps[r, :].rearrange("p (a t) -> p a t", t=TB),
                                                   ACT.Identity, bias=small_sb[r, C_BQ:C_BQ + 1])
                            ins.then_inc(q_ev, 1)
                        if g == 2 and m3.exists():
                            a.wait_ge(z_mm, m3.p + 1)
                            a.copy(row(z_all, m3), a_ps[:]).then_inc(z_ev, 1)
                        if g == 2 and s1.exists():
                            a.wait_ge(k_mm, s1.p + 1)
                            if s1.fixed and s1.p == 0:
                                a.wait_ge(gain_rdy, 3)
                                a.wait_ge(const_ld, 16)
                            for h in range(V):
                                ins = a.activation(k_bd[s1.b][:, h, PAD:PAD + T], b_ps[:], ACT.Identity,
                                                   scale=head_mask[:, h:h + 1], bias=bk_head[:, h:h + 1])
                            ins.then_inc(k_ev, 1)
                        if g == 3 and s1.exists():
                            a.wait_ge(v_mm, s1.p + 1)
                            if s1.at(-2).exists():
                                a.wait_ge(vt, s1.p - 1)
                            a.activation(v_sb[s1.b][:, PAD:PAD + T], a_ps[:], ACT.Identity,
                                         bias=small_sb[:, C_BV:C_BV + 1]).then_inc(v_ev, 1)
                        if n.at(-1).exists():
                            m = n.at(-1)
                            a.wait_ge(sub, m.n + 1)
                            if m.at(-2).exists():
                                a.wait_ge(tr, m.n - 1)
                            a.activation(prob[m.b][:, :, 0:KW],
                                         s_ps[m.b][:, :, 0:2 * V * KW].rearrange("p h (a k) -> p h a k", k=KW),
                                         ACT.Exp, scale=SCALE).then_inc(ex, 1)
                        if g == 3 and m2.exists():
                            a.wait_ge(xt_mm, m2.p + 1)
                            if m2.at(-2).exists():
                                a.wait_ge(z_mm, m2.p - 1)
                            a.copy(xr_t[m2.b][:], a_ps[:]).then_inc(xt_ev, 1)
                        if g == 0 and m2.exists():
                            a.wait_ge(st2, m2.p + 1)
                            if m2.at(-2).exists():
                                a.wait_ge(xn2_rdy, m2.p - 1)
                            a.activation(ln2[m2.b][:, 0:1], mv2[m2.b][:, 1:2], ACT.Ln, bias=LN_EPS).then_inc(ln2_a, 1)
                            a.wait_ge(ln2_a, m2.p + 1)
                            a.activation(ln2[m2.b][:, 1:2], ln2[m2.b][:, 0:1], ACT.Exp, scale=-0.5).then_inc(y2, 1)
                        if n.at(-3).exists():
                            m = n.at(-3)
                            a.wait_ge(pv, m.n + 1)
                            if m.at(-2).exists():
                                a.wait_ge(rd, m.n - 1)
                            o_all = o_ps[:, :, 0:U * VW].rearrange("p e (u w) -> p e u w", w=VW)
                            a.copy(den[m.b][:], o_all[:, :, :, TB]).then_inc(dn, 1)
                            if m.g == 0 and m.step.at(-2).exists():
                                a.wait_ge(oc, m.step.p - 1)
                            for h in range(V):
                                r = slice(TB * h, TB * h + TB)
                                dst = o_t[m.step.b][r, m.g * GT * U:(m.g + 1) * GT * U, :]
                                ins = a.copy(dst.rearrange("p (e u) d -> p e u d", u=U),
                                             o_all[r, :, :, h * HD:(h + 1) * HD])
                            ins.then_inc(ov, 1)
                        if g == 2 and s2.exists():
                            a.wait_ge(st1, s2.p + 1)
                            if s.exists():
                                a.wait_ge(xn_rdy, s.p + 1)
                            a.activation(ln1[s2.b][:, 0:1], mv1[s2.b][:, 1:2], ACT.Ln, bias=LN_EPS).then_inc(ln1_a, 1)
                            a.wait_ge(ln1_a, s2.p + 1)
                            a.activation(ln1[s2.b][:, 1:2], ln1[s2.b][:, 0:1], ACT.Exp, scale=-0.5).then_inc(y1, 1)

                done = [0]

                def answer(ins):
                    done[0] += 1
                    ins.then_inc(act_b, 1)
                    return done[0]

                def after(name):
                    a.wait_ge(vec_b, VB[name])

                def ln_exp(src, bias):
                    a.wait_ge(act_b, answer(a.activation(tok[:, 0, :], src, ACT.Ln, bias=bias)))
                    answer(a.activation(tok[:, 1, :], tok[:, 0, :], ACT.Exp, scale=-0.5))

                def deviations():
                    a.wait_ge(mvc, PAIRS)
                    ln_exp(mv_all[:, :, 1], LN_EPS)
                    after("w")
                    ln_exp(tok[:, 7, :], 0.0)

                run_pairs(a, pair, before_last=deviations)
                after("z_sub")
                answer(a.activation(e4[:], m4[:], ACT.Exp, scale=1.0 / TAU))
                after("gates_sub")
                answer(a.activation(gates[:], gates[:], ACT.Exp))
                after("row_sum")
                answer(a.activation(lns[:], sums[:], ACT.Ln))
                after("col_sub")
                answer(a.activation(e4[:], m4[:], ACT.Exp))
                after("col_sum")
                answer(a.activation(lns[:], sums[:], ACT.Ln))
                after("col_ln")
                answer(a.activation(m4[:], m4[:], ACT.Exp, bias=LN_LIFT))

                def logs(k, n):
                    g = streams[k]
                    a.wait_ge(red[k], n + 1)
                    a.activation(lns[:, g], sums[:, g], ACT.Ln, scale=1.0 / LIFT).then_inc(lnd[k], 1)

                def reciprocals(k, n):
                    g = streams[k]
                    a.wait_ge(lnd[k], n + 1)
                    a.activation(recs[:, g], lns[:, g], ACT.Exp, scale=-1.0).then_inc(rec[k], 1)

                def iteration(it):
                    for half in range(2):
                        n = it * 2 + half
                        logs(0, n)
                        logs(1, n)
                        reciprocals(0, n)
                        reciprocals(1, n)
                        logs(2, n)
                        reciprocals(2, n)

                def copy_branch(s):
                    a.wait_ge(gz_mm, s.p + 1)
                    a.copy(row(z_all, s), m_ps[s.b]).then_inc(gz_ev, 1)

                def seven(i, copies=False):
                    for it in range(UNROLL):
                        iteration(i * UNROLL + it)
                        if copies and it % 2 == 0:
                            copy_branch(Step(i, it // 2 - 8, 4))

                seven(0)
                a.wait_ge(g_mv, 1)
                a.copy(flat(g_row), a_ps[:, 0:QT * PAIRS * NG1]).then_inc(g_row_rdy, 1)
                seven(1)
                with a.Fori(2, 2 + PAIRS // 4) as i:
                    seven(i, copies=True)
                for i in range(2 + PAIRS // 4, (ITERS - 1) // UNROLL):
                    seven(i)
                a.wait_ge(h_mv, 1)
                a.copy(flat(h_row), b_ps[:, 0:QT * PAIRS * NS]).then_inc(h_row_rdy, 1)

            @block.gpsimd
            def _(pool):
                pool.memset(q_bd[0][:], 0.0).then_inc(zeroed, 1)

                def pair(s):
                    m1 = s.at(-1)
                    for g in range(NG):
                        n = Group(s, g)
                        if n.exists():
                            pool.wait_ge(mx, n.n + 1)
                            if n.at(-2).exists():
                                pool.wait_ge(sub, n.n - 1)
                            settle(pool)
                            pool.tensor_copy(nm_hi[n.b][:], negmax[n.b][:]).then_inc(hi, 1)
                            pool.wait_ge(hi, n.n + 1)
                            pool.tensor_tensor(nm_lo[n.b][:], negmax[n.b][:], nm_hi[n.b][:],
                                               ALU.subtract).then_inc(lo, 1)
                        if n.at(-3).exists():
                            m = n.at(-3)
                            pool.wait_ge(ov, m.n + 1)
                            pool.wait_ge(rd, m.n + 1)
                            o = o_t[m.step.b][:, m.g * GT * U:(m.g + 1) * GT * U, :]
                            pool.tensor_tensor(o, o, rden[m.b][:].rearrange("p e u -> p (e u)").unsqueeze(2)
                                               .broadcast_to([P, GT * U, HD]), ALU.mult).then_inc(nrm, 1)
                        if g == 1 and m1.exists():
                            if m1.fixed and m1.p == 0:
                                pool.wait_ge(gain_rdy, 3)
                            pool.wait_ge(r_ld[m1.b], m1.uses * 16)
                            settle(pool)
                            pool.tensor_scalar(x_res[m1.b][:], x_res[m1.b][:], gains[:, 3:4], None,
                                               ALU.add).then_inc(xres, 1)

                run_pairs(pool, pair)

                def branch_coefficients(s):
                    if s.at(-2).exists():
                        pool.wait_ge(gz_mm, s.p - 1)
                    pool.tensor_tensor(gbd[s.b][:], tok_mask, own_token(g_row, s), ALU.mult).then_inc(g_rdy, 1)
                    if s.at(-2).exists():
                        add_mean(s.at(-2))

                def add_mean(s):
                    pool.wait_ge(gz_ev, s.p + 1)
                    y = tiles(row(z_all, s))
                    pool.tensor_tensor(y, y, of_pair(g_row, s, slice(NS, NG1)).broadcast_to([P, QT, DIM]),
                                       ALU.add).then_inc(y_rdy, 1)

                pool.wait_ge(g_row_rdy, 1)
                run_mix(pool, branch_coefficients)
                for c in range(2):
                    add_mean(Step(PAIRS // 2 - 1, c))

                pool.wait_ge(h_row_rdy, 1)
                pool.wait_ge(gz_mm, PAIRS)

                def row_coefficients(s):
                    if s.b == 1:
                        if s.at(-4).exists():
                            pool.wait_ge(hx_mm, s.p - 3)
                        pool.tensor_tensor(h_bd[s.c % 4][:], tok_mask, own_token(h_row, s), ALU.mult)\
                            .then_inc(h_rdy[1], 1)

                run_mix(pool, row_coefficients, 4)


VB = {"w": 10, "z_sub": 18, "gates_sub": 20, "row_sum": 21, "col_sub": 24, "col_sum": 27, "col_ln": 30, "g": 32, "h": 34}


def kernel(**inputs):
    import concourse.bacc as bacc
    from concourse.bass_utils import run_bass_kernel_spmd

    a = {k: np.asarray(val) for k, val in inputs.items()}
    f32 = np.float32

    small = np.zeros((P, NSMALL), f32)
    for col, name in ((C_BQ, "bq"), (C_BK, "bk"), (C_BV, "bv"), (C_BO, "bo")):
        for b in range(2):
            small[b * C:(b + 1) * C, col] = a["L0_xattn_" + name]
    small[:, C_GX], small[:, C_GF], small[:, C_GATE] = a["g_xattn"][0], a["g_ffn"][0], a["L0_ffn_gate"][0]
    small[:, C_BASE:C_BASE + NS * NS] = a["L0_ffn_H_res_base"].reshape(1, -1)
    small[:, C_BASE + NS * NS:C_BASE + NS * NS + NS] = a["L0_ffn_H_pre_base"][None]
    small[:, C_BASE + NS * NS + NS:] = a["L0_ffn_H_post_base"][None]

    consts = np.zeros((P, NCONST), f32)
    for p in range(P):
        consts[p, K_ID + p] = 1.0
        t = p % TB
        consts[p, K_MASK:K_MASK + KW] = NEG
        consts[p, K_MASK + t:K_MASK + t + WINDOW] = 0.0
        consts[p, K_HEAD + (p // HD) % V] = 1.0
        consts[p, K_TOK + (p // NS) * NS:K_TOK + (p // NS) * NS + NS] = 1.0

    w4 = np.zeros((P, 4, P), f32)
    for b in range(2):
        r = slice(b * C, (b + 1) * C)
        for k, name in enumerate(("Wq", "Wk", "Wv")):
            w4[r, k, r] = a["L0_xattn_" + name].T
        for h in range(HEADS):
            to = (h % V) * U * HD + (b * (HEADS // V) + h // V) * HD
            w4[to:to + HD, 3, r] = a["L0_xattn_Wo"].T[h * HD:(h + 1) * HD]

    wl = np.concatenate([a["L0_ffn_W_res"], a["L0_ffn_W_pre"], a["L0_ffn_W_post"]])
    wl = np.ascontiguousarray(wl.reshape(NLOG, NS, DIM).transpose(2, 1, 0))

    pick_rows = np.zeros((P, NPICK), f32)
    pick_rows[np.arange(P), NS * np.arange(P) + NS - 1] = 1.0

    arrays = {"x": a["x"], "ctx": a["ctx_4096"], "small": small, "consts": consts, "pick": pick_rows, "w4": w4, "wl": wl,
              "wb": a["L0_ffn_W_branch"]}
    nc = bacc.Bacc("TRN2", target_bir_lowering=False, num_devices=1)
    aps = [nc.dram_tensor(k, val.shape, F32, kind="ExternalInput").ap() for k, val in arrays.items()]
    out = nc.dram_tensor("out", (B, C, T), F32, kind="ExternalOutput").ap()
    xn_dram = nc.dram_tensor("xn_scratch", (NTOK, T), F32, kind="Internal").ap()
    build(nc, *aps, out, xn_dram)
    r = run_bass_kernel_spmd(nc, [{k: np.ascontiguousarray(val) for k, val in arrays.items()}], core_ids=[0])
    return r.results[0]["out"]
```

```python
from contextlib import ExitStack

import numpy as np
import concourse.bass as bass
from concourse import mybir

F32 = mybir.dt.float32
BF16 = mybir.dt.bfloat16
ALU = mybir.AluOpType
ACT = mybir.ActivationFunctionType
AX = mybir.AxisListType

P = 128
B, C, T = 32, 64, 512
HEADS, WINDOW = 8, 16
HD = C // HEADS
SCALE = float(HD) ** -0.5
PAD = WINDOW // 2
U, V = 4, 4
TB = 32
NTB = T // TB
KW = 48
NBLK = NTB + 1
TP = NBLK * TB
VW = TB + 1
PAIRS = B // 2
GT = 4
NG = NTB // GT
GROUPS = PAIRS * NG
NS, DIM = 4, 128
NTOK = B * C
TILES = NTOK * NS // P
QT = P // TB
NLOG = NS * NS + 2 * NS
NG1 = NS + 1
ITERS = 50
TAU = 0.1
LN_EPS = 1e-5
RMS_EPS = 1.1920929e-07
NEG = -1e30
LIFT = 2.0 ** 100
LN_LIFT = 100 * float(np.log(2.0))

C_BQ, C_BK, C_BV, C_BO, C_GX, C_GF, C_GATE, C_BASE = range(8)
NSMALL = C_BASE + NLOG
K_ID, K_MASK, K_TOK, K_HEAD = 0, P, P + KW, 2 * P + KW
NCONST = K_HEAD + V
NPICK = NS * P + 2 * (NS - 1)
HALVES = 2 * (ITERS - 1)
STREAMS = 3
KEPT = 4
LATE = 5
UNROLL = 7
assert (ITERS - 1) % UNROLL == 0


class Step:

    def __init__(self, i, c, per=2):
        self.i, self.c, self.per, self.fixed = i, c, per, isinstance(i, int)

    def at(self, off):
        return Step(self.i, self.c + off, self.per)

    def exists(self):
        return not self.fixed or 0 <= self.p < PAIRS

    @property
    def p(self):
        return self.i * self.per + self.c

    @property
    def b(self):
        return self.c % 2

    @property
    def uses(self):
        return self.i * (self.per // 2) + (self.c // 2 + 1)


class Group:

    def __init__(self, step, g):
        self.step, self.g = step.at(g // NG), g % NG

    def at(self, off):
        return Group(self.step, self.g + off)

    def exists(self):
        return self.step.exists()

    @property
    def n(self):
        return self.step.i * (2 * NG) + (self.step.c * NG + self.g)

    @property
    def b(self):
        return self.g % 2


def build(nc, x, ctxin, small, consts, pick_rows, w4, wl, wb, out, xn_dram):
    with ExitStack() as ctx:
        def sb(name, shape, dt=F32):
            return ctx.enter_context(nc.sbuf_tensor(name, shape, dt))

        def pb(name, shape):
            return ctx.enter_context(nc.psum_tensor(name, shape, F32))

        def sem(name):
            return ctx.enter_context(nc.semaphore(name))

        def sem2(name):
            return [sem(f"{name}{b}") for b in range(2)]

        small_sb = sb("small_sb", [P, NSMALL])
        consts_sb = sb("consts_sb", [P, NCONST])
        pick_sb = sb("pick_sb", [P, NPICK])
        w4_sb = sb("w4_sb", [P, 4, P])
        wl_sb = sb("wl_sb", [P, NS, NLOG])
        wb_sb = sb("wb_sb", [P, DIM])
        ident = consts_sb[:, K_ID:K_ID + P]
        head_mask = consts_sb[:, K_HEAD:K_HEAD + V]
        ident_bf = sb("ident_bf", [P, P], BF16)
        mask_bf = sb("mask_bf", [P, KW], BF16)
        gains = sb("gains", [P, 8])
        bk_head = sb("bk_head", [P, V])
        x_in = [sb(f"x_in{b}", [P, T]) for b in range(2)]
        ctx_in = [sb(f"ctx_in{b}", [P, T]) for b in range(2)]
        x_res = [sb(f"x_res{b}", [P, T]) for b in range(2)]
        xn = [sb(f"xn{b}", [P, T]) for b in range(2)]
        v_sb = [sb(f"v_sb{b}", [P, TP]) for b in range(2)]
        q_bd = [sb(f"q_bd{b}", [P, NTB, U, TB]) for b in range(2)]
        k_bd = [sb(f"k_bd{b}", [P, V, TP]) for b in range(2)]
        v_t = [sb(f"v_t{b}", [P, NBLK, VW]) for b in range(2)]
        v_bd = [sb(f"v_bd{b}", [P, U, NBLK, VW]) for b in range(2)]
        stats1 = sb("stats1", [P, 6])
        mv1 = [sb(f"mv1_{b}", [P, 2]) for b in range(2)]
        ln1 = [sb(f"ln1_{b}", [P, 4]) for b in range(2)]
        negmax = [sb(f"negmax{b}", [P, GT * V]) for b in range(2)]
        prob = [sb(f"prob{b}", [P, GT * V, 2 * TB]) for b in range(2)]
        prob_t = [sb(f"prob_t{b}", [P, 2, GT, P]) for b in range(2)]
        den = [sb(f"den{b}", [P, GT, U]) for b in range(2)]
        rden = [sb(f"rden{b}", [P, GT, U]) for b in range(2)]
        o_t = [sb(f"o_t{b}", [P, NTB * U, HD]) for b in range(2)]
        o_c = [sb(f"o_c{b}", [P, T]) for b in range(2)]
        x2 = [sb(f"x2_{b}", [P, T]) for b in range(2)]
        stats2 = sb("stats2", [P, 6])
        mv2 = [sb(f"mv2_{b}", [P, 2]) for b in range(2)]
        ln2 = [sb(f"ln2_{b}", [P, 4]) for b in range(2)]
        xn2 = [sb(f"xn2_{b}", [P, T]) for b in range(2)]
        mv_all = sb("mv_all", [P, PAIRS, 2])
        xr_all = sb("xr_all", [P, PAIRS, QT * DIM])
        xr_t = [sb(f"xr_t{b}", [P, QT * P]) for b in range(2)]
        z_all = sb("z_all", [P, PAIRS, QT * DIM])
        logit = sb("logit", [P, PAIRS, NLOG])
        hbd = [sb(f"hbd{b}", [P, QT, TB, NS]) for b in range(2)]
        gbd = [sb(f"gbd{b}", [P, QT, TB, NS]) for b in range(2)]
        h_tok = sb("h_tok", [P, PAIRS, NS, NS])
        g_tok = sb("g_tok", [P, PAIRS, NS, NG1])
        h_row = sb("h_row", [P, QT, PAIRS, NS])
        g_row = sb("g_row", [P, QT, PAIRS, NG1])
        tok = sb("tok", [P, 8, PAIRS])
        gates = sb("gates", [P, PAIRS, 2, NS])
        gates_m = sb("gates_m", [P, 2, PAIRS, 2])
        m4 = sb("m4", [P, PAIRS, NS, NS])
        e4 = sb("e4", [P, PAIRS, NS, NS])
        sums = sb("sums", [P, PAIRS, NS])
        lns = sb("lns", [P, PAIRS, NS])
        recs = sb("recs", [P, PAIRS, NS])
        s_ps = [pb(f"s_ps{b}", [P, 2, 512]) for b in range(2)]
        o_ps = pb("o_ps", [P, GT, 256])
        l_ps = o_ps[:, 0, U * VW:U * VW + NLOG]
        a_ps = pb("a_ps", [P, 512])
        b_ps = pb("b_ps", [P, 512])
        m_ps = [s_ps[0][:, 0, :], s_ps[1][:, 0, :], s_ps[0][:, 1, :], s_ps[1][:, 1, :]]

        NZERO = 13

        small_ld, w_ld, const_ld, wf_ld = (sem(s) for s in ("small_ld", "w_ld", "const_ld", "wf_ld"))
        zeroed, cleared, const_rdy, gain_rdy, settled = (
            sem(s) for s in ("zeroed", "cleared", "const_rdy", "gain_rdy", "settled"))
        act_g, vec_g = sem("act_g"), sem("vec_g")
        x_ld, c_ld, r_ld = sem2("x_ld"), sem2("c_ld"), sem2("r_ld")
        vx, xn_st = sem2("vx"), sem2("xn_st")
        st1_raw, st1, ln1_a, y1, nw1, xn_rdy = (sem(s) for s in ("st1_raw", "st1", "ln1_a", "y1", "nw1", "xn_rdy"))
        q_mm, k_mm, v_mm, q_ev, k_ev, v_ev, vt = (sem(s) for s in ("q_mm", "k_mm", "v_mm", "q_ev", "k_ev", "v_ev", "vt"))
        mk, sc, mx, sub, ex, tr, pv, dn, rd, ov, nrm = (
            sem(s) for s in ("mk", "sc", "mx", "sub", "ex", "tr", "pv", "dn", "rd", "ov", "nrm"))
        oc, wo, xres, x2_rdy = sem("oc"), sem("wo"), sem("xres"), sem("x2_rdy")
        st2_raw, st2, mvc, ln2_a, y2, nw2, xn2_rdy = (
            sem(s) for s in ("st2_raw", "st2", "mvc", "ln2_a", "y2", "nw2", "xn2_rdy"))
        xt_mm, xt_ev, l_mm, l_ev, z_mm, z_ev = (sem(s) for s in ("xt_mm", "xt_ev", "l_mm", "l_ev", "z_mm", "z_ev"))

        vec_b, act_b = sem("vec_b"), sem("act_b")
        pick_ld, g_mv, g_row_rdy, h_mv, h_row_rdy = (sem(s) for s in ("pick_ld", "g_mv", "g_row_rdy", "h_mv", "h_row_rdy"))
        red, lnd, rec, mul = ([sem(f"{s}{k}") for k in range(STREAMS)] for s in ("red", "lnd", "rec", "mul"))
        xr_all_ld, out_st = sem("xr_all_ld"), sem("out_st")
        g_rdy, gz_mm, gz_ev, y_rdy = sem("g_rdy"), sem("gz_mm"), sem("gz_ev"), sem("y_rdy")
        h_rdy, hx_mm, out_rdy = sem2("h_rdy"), sem("hx_mm"), sem("out_rdy")

        def settle(eng):
            eng.sem_inc(settled, 1)

        def run_pairs(eng, program, after_first=lambda: None):
            program(Step(-1, 0))
            after_first()
            program(Step(-1, 1))
            for i in (0, 1):
                for c in range(2):
                    program(Step(i, c))
            with eng.Fori(2, PAIRS // 2 - 1) as i:
                for c in range(2):
                    program(Step(i, c))
            for i in (PAIRS // 2 - 1, PAIRS // 2):
                for c in range(2):
                    program(Step(i, c))
            program(Step(PAIRS // 2 + 1, 0))

        def row(t, s):
            return t[:, bass.ds(s.p, 1), :].rearrange("p a n -> p (a n)")

        x_pair = x.rearrange("(q b) c t -> q (b c) t", b=2)
        ctx_pair = ctxin.rearrange("(q b) c t -> q (b c) t", b=2)
        xn_pair = xn_dram.rearrange("(q r) n -> q r n", r=P)
        xn_tile = xn_dram.rearrange("(q t r) (j n) -> q (r j) t n", t=QT, r=TB, j=NS)

        def pick(ap, s):
            return ap[bass.ds(s.p, 1)].rearrange("a r n -> (a r) n")

        def pick_tile(ap, s):
            return ap[bass.ds(s.p, 1)].rearrange("a r t n -> (a r) t n")

        cuts = [PAIRS * k // STREAMS for k in range(STREAMS + 1)]
        streams = [slice(cuts[k], cuts[k + 1]) for k in range(STREAMS)]
        whole = slice(0, PAIRS)

        def over_j(t, g):
            return t[:, g].unsqueeze(3).broadcast_to([P, g.stop - g.start, NS, NS])

        def over_i(t, g):
            return t[:, g].unsqueeze(2).broadcast_to([P, g.stop - g.start, NS, NS])

        def cols(t, g):
            return t[:, g].rearrange("p a i j -> p a j i")

        def flat(t):
            return t[:].rearrange("p a b -> p (a b)") if len(t.shape) == 3 else t[:].rearrange("p a b c -> p (a b c)")

        out_rows = out.rearrange("b c n -> (b c) n").rearrange("(q t r) (j n) -> q (r j) t n", t=QT, r=TB, j=NS)
        h_bd = hbd + gbd
        tok_mask = consts_sb[:, K_TOK:K_TOK + P].rearrange("p (t i) -> p t i", i=NS).unsqueeze(1)\
            .broadcast_to([P, QT, TB, NS])

        def run_mix(eng, program, per=2, peeled=1):
            for i in range(peeled):
                for c in range(per):
                    program(Step(i, c, per))
            with eng.Fori(peeled, PAIRS // per) as i:
                for c in range(per):
                    program(Step(i, c, per))

        def run_branch(eng, program):
            for c in range(2):
                program(Step(KEPT // 2, c))
            with eng.Fori(KEPT // 2 + 1, PAIRS // 2) as i:
                for c in range(2):
                    program(Step(i, c))

        def of_pair(t, s, cols):
            return t[:, :, bass.ds(s.p, 1), cols].rearrange("p t a k -> p t (a k)")

        def own_token(t, s):
            return of_pair(t, s, slice(0, NS)).unsqueeze(2).broadcast_to([P, QT, TB, NS])

        def tiles(t):
            return t.rearrange("p (t n) -> p t n", t=QT)

        def refine_and_apply(eng, s, mv, ln, step, src, dst, done, ready=lambda eng: None):
            var, y, t = mv[:, 1:2], ln[:, 1:2], ln[:, 2:3]
            ready(eng)
            eng.tensor_scalar(t, var, LN_EPS, y, ALU.add, ALU.mult).then_inc(step, 1)
            eng.wait_ge(step, s.p * 3 + 1)
            ready(eng)
            eng.tensor_scalar(ln[:, 3:4], t, y, -0.5, ALU.mult, ALU.mult).then_inc(step, 1)
            eng.wait_ge(step, s.p * 3 + 2)
            ready(eng)
            eng.tensor_scalar(t, ln[:, 3:4], 1.5, y, ALU.add, ALU.mult).then_inc(step, 1)
            eng.wait_ge(step, s.p * 3 + 3)
            ready(eng)
            eng.tensor_scalar(dst, src, mv[:, 0:1], t, ALU.subtract, ALU.mult).then_inc(done, 1)

        def normalise_input(eng, s2):
            eng.wait_ge(y1, s2.p + 1)
            if s2.at(-2).exists():
                eng.wait_ge(q_mm, s2.p - 1)
            refine_and_apply(eng, s2, mv1[s2.b], ln1[s2.b], nw1, x_in[s2.b][:], xn[s2.b][:], xn_rdy, settle)

        with nc.Block() as block:

            @block.sync
            def _(sp):
                def load_x(s):
                    sp.dma_start(x_in[s.b][:], pick(x_pair, s)).then_inc(x_ld[s.b], 16)

                def load_ctx(s):
                    sp.dma_start(ctx_in[s.b][:], pick(ctx_pair, s)).then_inc(c_ld[s.b], 16)

                load_x(Step(0, 0))
                sp.dma_start(small_sb[:], small).then_inc(small_ld, 16)
                sp.dma_start(w4_sb[:], w4).then_inc(w_ld, 16)
                load_ctx(Step(0, 0))
                sp.dma_start(consts_sb[:], consts).then_inc(const_ld, 16)
                load_x(Step(0, 1))
                load_ctx(Step(0, 1))
                sp.dma_start(wl_sb[:], wl).then_inc(wf_ld, 16)
                sp.dma_start(wb_sb[:], wb).then_inc(wf_ld, 16)
                sp.dma_start(pick_sb[:], pick_rows).then_inc(pick_ld, 16)

                def pair(s):
                    s2, s1, m1, m2 = s.at(2), s.at(1), s.at(-1), s.at(-2)
                    if s2.exists() and s.exists():
                        sp.wait_ge(xn_rdy, s.p + 1)
                        load_x(s2)
                        sp.wait_ge(v_mm, s.p + 1)
                        settle(sp)
                        load_ctx(s2)
                    if s.exists():
                        if m2.exists():
                            sp.wait_ge(x2_rdy, m2.p + 1)
                            settle(sp)
                        sp.dma_start(x_res[s.b][:], pick(x_pair, s)).then_inc(r_ld[s.b], 16)
                    if m2.exists():
                        sp.wait_ge(xn2_rdy, m2.p + 1)
                        sp.dma_start(pick(xn_pair, m2), xn2[m2.b][:]).then_inc(xn_st[m2.b], 16)
                    if s1.exists():
                        sp.wait_ge(vt, s1.p + 1)
                        settle(sp)
                        last = Group(s1.at(-2), NG - 1)
                        if s1.fixed and s1.p == 0:
                            sp.wait_ge(cleared, 3)
                        if last.exists():
                            sp.wait_ge(pv, last.n + 1)
                        for u in range(U):
                            r = slice(TB * u, TB * u + TB)
                            sp.dma_start(v_bd[s1.b][r, u, :, :], v_t[s1.b][r, :, :]).then_inc(vx[s1.b], 16)

                run_pairs(sp, pair)

                for stored in xn_st:
                    sp.wait_ge(stored, 16 * PAIRS // 2)
                for k in range(4):
                    q = slice(k * PAIRS // 4, (k + 1) * PAIRS // 4)
                    sp.dma_start(xr_all[:, q].rearrange("p q (t n) -> p q t n", t=QT),
                                 xn_tile[q].rearrange("q p t n -> p q t n")).then_inc(xr_all_ld, 16)

                def store(s):
                    sp.wait_ge(out_rdy, s.p + 1)
                    settle(sp)
                    sp.dma_start(pick_tile(out_rows, s), tiles(row(z_all, s))).then_inc(out_st, 16)

                run_mix(sp, store)
                sp.wait_ge(out_st, 16 * PAIRS)

            @block.tensor
            def _(pe):
                pe.wait_ge(w_ld, 16)

                def scores(n):
                    s = n.step
                    if n.g == 0 and s.fixed and s.p == 0:
                        pe.wait_ge(const_rdy, 2)
                        pe.wait_ge(zeroed, NZERO)
                        pe.wait_ge(const_ld, 16)
                    if n.g == 0:
                        pe.wait_ge(q_ev, s.p + 1)
                        pe.wait_ge(k_ev, s.p + 1)
                    first = n.step.fixed and n.n < 2
                    if not first:
                        pe.wait_ge(mk, n.n - 1)
                    for h in range(2):
                        if first:
                            pe.matmul(s_ps[n.b][:, h, 0:2 * V * KW], ident_bf[:],
                                      mask_bf[:].unsqueeze(1).broadcast_to([P, 2 * V, KW]),
                                      start=True, stop=False, skip_group_check=True)
                        for e in range(2):
                            tb = n.g * GT + 2 * h + e
                            t0 = tb * TB
                            mm = pe.matmul(s_ps[n.b][:, h, e * V * KW:(e + 1) * V * KW],
                                           q_bd[s.b][:, tb].rearrange("p u t -> p (u t)"),
                                           k_bd[s.b][:, :, t0:t0 + KW], start=False, stop=(e == 1), skip_group_check=True)
                    mm.then_inc(sc, 1)

                def values(n):
                    s = n.step
                    if n.g == 0:
                        pe.wait_ge(vx[s.b], s.uses * 16 * U)
                    pe.wait_ge(tr, n.n + 1)
                    if n.at(-1).exists():
                        pe.wait_ge(ov, n.n)
                    for e in range(GT):
                        for k in range(2):
                            mm = pe.matmul(o_ps[:, e, 0:U * VW], prob_t[n.b][:, k, e, :],
                                           v_bd[s.b][:, :, n.g * GT + e + k, :], start=(k == 0), stop=(k == 1))
                    mm.then_inc(pv, 1)

                def rows_transposed(m, s1):
                    pe.wait_ge(xn2_rdy, m.p + 1)
                    if s1.exists():
                        pe.wait_ge(v_ev, s1.p + 1)
                    else:
                        pe.wait_ge(z_ev, m.p)
                    for j in range(NS):
                        mm = pe.transpose(a_ps[:, j * P:(j + 1) * P], xn2[m.b][:, j * P:(j + 1) * P], ident)
                    mm.then_inc(xt_mm, 1)

                def logits(m, outputs):
                    if m.fixed and m.p == 0:
                        pe.wait_ge(wf_ld, 32)
                    pe.wait_ge(xt_ev, m.p + 1)
                    pe.wait_ge(ov, outputs)
                    for j in range(NS):
                        mm = pe.matmul(l_ps, xr_t[m.b][:, j:QT * P:NS], wl_sb[:, j, :],
                                       start=(j == 0), stop=(j == NS - 1))
                    mm.then_inc(l_mm, 1)

                def branch(m, s1):
                    if s1.exists():
                        pe.wait_ge(q_ev, s1.p + 1)
                    for t in range(QT):
                        mm = pe.matmul(a_ps[:, t * DIM:(t + 1) * DIM], xr_t[m.b][:, t * P:(t + 1) * P], wb_sb[:],
                                       start=True, stop=True)
                    mm.then_inc(z_mm, 1)

                def pair(s):
                    s1, m1, m2, m3 = s.at(1), s.at(-1), s.at(-2), s.at(-3)
                    for g in range(NG):
                        n = Group(s, g)
                        if n.exists():
                            scores(n)
                        draining = s.fixed and s.p >= PAIRS
                        if g == 1 and m3.exists() and not draining:
                            logits(m3, Group(m3, 3 * NG - 2).n + 1)
                        if n.at(-2).exists():
                            values(n.at(-2))
                        if g == 1 and m3.exists() and draining:
                            logits(m3, GROUPS)
                        if g == 3 and m2.exists() and not draining:
                            rows_transposed(m2, s1)
                        if g == 3 and m1.exists():
                            pe.wait_ge(oc, m1.p + 1)
                            if s1.exists():
                                pe.wait_ge(k_ev, s1.p + 1)
                            pe.matmul(b_ps[:], w4_sb[:, 3, :], o_c[m1.b][:], start=True, stop=True).then_inc(wo, 1)
                        if g == 3 and m2.exists() and draining:
                            rows_transposed(m2, s1)
                        if g == 0 and s1.exists():
                            pe.wait_ge(xn_rdy, s1.p + 1)
                            if m3.exists():
                                pe.wait_ge(xt_ev, m3.p + 1)
                            elif s.exists():
                                pe.wait_ge(v_ev, s.p + 1)
                            pe.matmul(a_ps[:], w4_sb[:, 0, :], xn[s1.b][:], start=True, stop=True).then_inc(q_mm, 1)
                        if g == 1 and s1.exists():
                            pe.wait_ge(c_ld[s1.b], s1.uses * 16)
                            if m2.exists():
                                pe.wait_ge(x2_rdy, m2.p + 1)
                            elif s.exists():
                                pe.wait_ge(k_ev, s.p + 1)
                            pe.matmul(b_ps[:], w4_sb[:, 1, :], ctx_in[s1.b][:], start=True, stop=True).then_inc(k_mm, 1)
                        if g == 1 and m3.exists():
                            branch(m3, s1)
                        if g == 2 and s1.exists():
                            if m3.exists():
                                pe.wait_ge(z_ev, m3.p + 1)
                            else:
                                pe.wait_ge(q_ev, s1.p + 1)
                            pe.matmul(a_ps[:], w4_sb[:, 2, :], ctx_in[s1.b][:], start=True, stop=True).then_inc(v_mm, 1)

                run_pairs(pe, pair)
                pe.wait_ge(sub, GROUPS)
                pe.wait_ge(z_ev, PAIRS)
                pe.wait_ge(l_ev, PAIRS)

                def to_rows(src, n, dst, done):
                    for t in range(QT):
                        for j in range(NS):
                            c0 = t * P + NS - 1 - j
                            mm = pe.matmul(dst[:, t * PAIRS * n:(t + 1) * PAIRS * n].rearrange("p (a k) -> p a k", k=n),
                                           pick_sb[:, c0:c0 + P], src[:, :, j, :], start=(j == 0), stop=(j == NS - 1))
                    mm.then_inc(done, 1)

                def branch_mixed(s):
                    pe.wait_ge(g_rdy, s.p - (KEPT - 1))
                    if not (s.fixed and s.p < KEPT + 2):
                        pe.wait_ge(gz_ev, s.p - (KEPT + 1))
                    branch_products(m_ps[s.b], gbd[s.b], s, True)

                def branch_products(dst, coefficients, s, stop):
                    for t in range(QT):
                        mm = pe.matmul(dst[:, t * DIM:(t + 1) * DIM], coefficients[:, t].rearrange("p a i -> p (a i)"),
                                       row(z_all, s)[:, t * DIM:(t + 1) * DIM], start=stop or t == 0, stop=stop,
                                       skip_group_check=True)
                    mm.then_inc(gz_mm, 1)

                def rows_mixed(s):
                    pe.wait_ge(h_rdy[s.b], s.uses)
                    if s.at(-4).exists():
                        pe.wait_ge(out_rdy, s.p - 3)
                    for t in range(QT):
                        mm = pe.matmul(m_ps[s.c % 4][:, t * DIM:(t + 1) * DIM],
                                       h_bd[s.c % 4][:, t].rearrange("p a i -> p (a i)"),
                                       row(xr_all, s)[:, t * DIM:(t + 1) * DIM], start=not (s.fixed and s.p < KEPT),
                                       stop=True, skip_group_check=True)
                    mm.then_inc(hx_mm, 1)

                pe.wait_ge(pick_ld, 16)
                pe.wait_ge(vec_b, VB["g"])
                to_rows(g_tok, NG1, a_ps, g_mv)
                run_branch(pe, branch_mixed)
                pe.wait_ge(gz_ev, PAIRS - KEPT)
                pe.wait_ge(mul[STREAMS - 1], HALVES - LATE)
                for c in range(KEPT):
                    pe.wait_ge(g_rdy, PAIRS - KEPT + c + 1)
                    branch_products(m_ps[c], h_bd[c], Step(0, c, KEPT), False)
                pe.wait_ge(vec_b, VB["h"])
                to_rows(h_tok, NS, b_ps, h_mv)
                pe.wait_ge(xr_all_ld, 16 * 4)
                run_mix(pe, rows_mixed, 4)

            @block.vector
            def _(v):
                for t in k_bd:
                    v.memset(t[:, :, 0:PAD], 0.0).then_inc(zeroed, 1)
                    v.memset(t[:, :, PAD + T:TP], 0.0).then_inc(zeroed, 1)
                for t in v_sb:
                    v.memset(t[:, 0:PAD], 0.0).then_inc(zeroed, 1)
                    v.memset(t[:, PAD + T:TP], 0.0).then_inc(zeroed, 1)
                for t in v_t:
                    v.memset(t[:, :, TB:VW], 1.0).then_inc(zeroed, 1)
                for t in prob:
                    v.memset(t[:, :, KW:2 * TB], 0.0).then_inc(zeroed, 1)

                def clear():
                    v.wait_ge(const_ld, 16)
                    v.tensor_copy(ident_bf[:], ident).then_inc(const_rdy, 1)
                    v.tensor_copy(mask_bf[:], consts_sb[:, K_MASK:K_MASK + KW]).then_inc(const_rdy, 1)
                    v.wait_ge(act_g, 3)
                    v.tensor_scalar(gains[:, 6:7], gains[:, 2:3], 1.0, None, ALU.add).then_inc(vec_g, 1)
                    v.wait_ge(vec_g, 1)
                    v.reciprocal(gains[:, 7:8], gains[:, 6:7]).then_inc(vec_g, 1)
                    v.wait_ge(vec_g, 2)
                    v.tensor_tensor(gains[:, 4:5], gains[:, 7:8], gains[:, 1:2], ALU.mult).then_inc(vec_g, 1)
                    v.wait_ge(vec_g, 3)
                    v.tensor_tensor(gains[:, 5:6], gains[:, 1:2], gains[:, 4:5], ALU.subtract).then_inc(gain_rdy, 1)
                    v.wait_ge(small_ld, 16)
                    v.tensor_tensor(gains[:, 3:4], gains[:, 0:1], small_sb[:, C_BO:C_BO + 1],
                                    ALU.mult).then_inc(gain_rdy, 1)
                    v.tensor_tensor(bk_head[:], head_mask, small_sb[:, C_BK:C_BK + 1].broadcast_to([P, V]),
                                    ALU.mult).then_inc(gain_rdy, 1)
                    v.wait_ge(gain_rdy, 3)
                    v.wait_ge(zeroed, NZERO)
                    for t in (v_bd[0], q_bd[1], v_bd[1]):
                        v.memset(t[:], 0.0).then_inc(cleared, 1)

                def pair(s):
                    s2, s1, m1, m2, m3 = s.at(2), s.at(1), s.at(-1), s.at(-2), s.at(-3)
                    for g in range(NG):
                        n = Group(s, g)
                        if g == 3 and s2.fixed and s2.p == 0:
                            normalise_input(v, s2)
                        if g == 2 and s.fixed and s.p == PAIRS + 1:
                            deviations()
                        if g == 3 and m1.exists():
                            v.wait_ge(nrm, m1.p * NG + NG)
                            if m1.at(-2).exists():
                                v.wait_ge(wo, m1.p - 1)
                            v.transpose(o_c[m1.b][:], o_t[m1.b][:].rearrange("p a d -> p (a d)")).then_inc(oc, 1)
                        if n.exists():
                            scores = s_ps[n.b][:, :, 0:2 * V * KW].rearrange("p h (a k) -> p h a k", k=KW)
                            v.wait_ge(sc, n.n + 1)
                            v.tensor_reduce(negmax[n.b][:].rearrange("p (h a) -> p h a", h=2), scores,
                                            AX.X, ALU.max, negate=True).then_inc(mx, 1)
                            v.wait_ge(mx, n.n + 1)
                            if n.at(-2).exists():
                                v.wait_ge(tr, n.n - 1)
                            v.tensor_tensor(prob[n.b][:, :, 0:KW].rearrange("p (h a) k -> p h a k", h=2), scores,
                                            negmax[n.b][:].rearrange("p (h a) -> p h a", h=2).unsqueeze(3)
                                            .broadcast_to([P, 2, 2 * V, KW]), ALU.add).then_inc(sub, 1)
                        if n.at(-3).exists():
                            m = n.at(-3)
                            v.wait_ge(dn, m.n + 1)
                            if m.at(-2).exists():
                                v.wait_ge(nrm, m.n - 1)
                            v.reciprocal(rden[m.b][:], den[m.b][:]).then_inc(rd, 1)
                        if n.at(-1).exists():
                            m = n.at(-1)
                            v.wait_ge(ex, m.n + 1)
                            if m.at(-2).exists():
                                v.wait_ge(pv, m.n - 1)
                            v.transpose(prob_t[m.b][:].rearrange("p k e (a t) -> p k (e a) t", t=TB),
                                        prob[m.b][:].rearrange("p a (k s) -> p k a s", k=2)).then_inc(tr, 1)
                        if g == 1 and m2.exists():
                            v.wait_ge(y2, m2.p + 1)
                            if m2.at(-2).exists():
                                v.wait_ge(xn_st[m2.b], (m2.uses - 1) * 16)
                                v.wait_ge(xt_mm, m2.p - 1)
                            refine_and_apply(v, m2, mv2[m2.b], ln2[m2.b], nw2, x2[m2.b][:], xn2[m2.b][:], xn2_rdy)
                        if g == 2 and s2.exists():
                            v.wait_ge(x_ld[s2.b], s2.uses * 16)
                            if s.at(1).exists():
                                v.wait_ge(st1, s2.p)
                            v.bn_stats(stats1[:], x_in[s2.b][:]).then_inc(st1_raw, 1)
                            v.wait_ge(st1_raw, s2.p + 1)
                            if s.exists():
                                v.wait_ge(xn_rdy, s.p + 1)
                            settle(v)
                            v.bn_aggr(mv1[s2.b][:], stats1[:]).then_inc(st1, 1)
                        if g == 3 and s1.exists():
                            v.wait_ge(v_ev, s1.p + 1)
                            if m1.exists():
                                v.wait_ge(vx[s1.b], (s1.uses - 1) * 16 * U)
                            v.transpose(v_t[s1.b][:, :, 0:TB], v_sb[s1.b][:].rearrange("p (a t) -> p a t", t=TB))\
                                .then_inc(vt, 1)
                        if g == 0 and m2.exists():
                            v.wait_ge(wo, m2.p + 1)
                            v.wait_ge(xres, m2.p + 1)
                            if m2.at(-2).exists():
                                v.wait_ge(xn2_rdy, m2.p - 1)
                            v.scalar_tensor_tensor(x2[m2.b][:], b_ps[:], gains[:, 0:1], x_res[m2.b][:],
                                                   ALU.mult, ALU.add).then_inc(x2_rdy, 1)
                            v.wait_ge(x2_rdy, m2.p + 1)
                            if m2.at(-2).exists():
                                v.wait_ge(mvc, m2.p - 1)
                            v.bn_stats(stats2[:], x2[m2.b][:]).then_inc(st2_raw, 1)
                            v.wait_ge(st2_raw, m2.p + 1)
                            settle(v)
                            v.bn_aggr(mv2[m2.b][:], stats2[:]).then_inc(st2, 1)

                n = [0]

                def link(ins, name=None):
                    n[0] += 1
                    ins.then_inc(vec_b, 1)
                    v.wait_ge(vec_b, n[0])
                    assert name is None or VB[name] == n[0], (name, n[0])

                def newton(arg, dst):
                    y, t, w = tok[:, 1, :], tok[:, 0, :], tok[:, 2, :]
                    link(v.tensor_tensor(t, arg, y, ALU.mult))
                    link(v.tensor_tensor(w, t, y, ALU.mult))
                    link(v.tensor_scalar(t, w, -0.5, 1.5, ALU.mult, ALU.add))
                    link(v.tensor_tensor(dst, t, y, ALU.mult))

                rstd, rrms, std, diag, w = (tok[:, k, :] for k in (3, 4, 5, 6, 7))
                var, mean = mv_all[:, :, 1], mv_all[:, :, 0]

                def deviations():
                    v.wait_ge(act_b, 2)
                    v.wait_ge(mvc, PAIRS)
                    link(v.tensor_scalar(w, var, LN_EPS, None, ALU.add))
                    newton(w, rstd)
                    link(v.tensor_tensor(std, w, rstd, ALU.mult))
                    link(v.tensor_scalar(diag, std, gains[:, 5:6], None, ALU.add))
                    link(v.tensor_tensor(tok[:, 0, :], var, rstd, ALU.mult))
                    link(v.tensor_tensor(tok[:, 1, :], tok[:, 0, :], rstd, ALU.mult))
                    link(v.tensor_scalar(w, tok[:, 1, :], RMS_EPS, None, ALU.add), "w")
                    v.wait_ge(act_b, 4)
                    newton(w, rrms)

                run_pairs(v, pair, clear)
                v.wait_ge(l_ev, PAIRS)
                link(v.tensor_tensor(logit[:], logit[:], rrms.unsqueeze(2).broadcast_to([P, PAIRS, NLOG]), ALU.mult))
                link(v.tensor_tensor(logit[:], logit[:], small_sb[:, C_BASE:C_BASE + NLOG].unsqueeze(1)
                                     .broadcast_to([P, PAIRS, NLOG]), ALU.add))
                zl = logit[:, :, 0:NS * NS].rearrange("p a (i j) -> p a i j", i=NS)
                link(v.tensor_reduce(sums[:], zl, AX.X, ALU.max))
                link(v.tensor_tensor(m4[:], zl, over_j(sums, whole), ALU.subtract), "z_sub")
                gl = logit[:, :, NS * NS:].rearrange("p a (k n) -> p a k n", k=2)
                gate_shape = [P, PAIRS, 2, NS]
                link(v.tensor_reduce(gates_m[:, 0], gl, AX.X, ALU.max))
                link(v.tensor_tensor(gates[:], gl, gates_m[:, 0].unsqueeze(3).broadcast_to(gate_shape), ALU.subtract),
                     "gates_sub")
                v.wait_ge(act_b, 5)
                link(v.tensor_reduce(sums[:], e4[:], AX.X, ALU.add), "row_sum")
                v.wait_ge(act_b, 7)
                m_rows = m4[:].rearrange("p a i j -> p (a i) j")
                link(v.scalar_tensor_tensor(m_rows, m_rows, 1.0 / TAU,
                                            flat(lns).unsqueeze(2).broadcast_to([P, PAIRS * NS, NS]),
                                            ALU.mult, ALU.subtract))
                link(v.tensor_reduce(sums[:], cols(m4, whole), AX.X, ALU.max))
                link(v.tensor_tensor(m4[:], m4[:], over_i(sums, whole), ALU.subtract), "col_sub")
                link(v.tensor_reduce(gates_m[:, 0], gates[:], AX.X, ALU.add))
                link(v.reciprocal(gates_m[:, 1], gates_m[:, 0]))
                v.wait_ge(act_b, 8)
                link(v.tensor_reduce(sums[:], cols(e4, whole), AX.X, ALU.add), "col_sum")
                link(v.tensor_tensor(gates[:], gates[:], gates_m[:, 1].unsqueeze(3).broadcast_to(gate_shape), ALU.mult))
                link(v.tensor_scalar(gates[:, :, 1, :], gates[:, :, 1, :], gains[:, 1:2], None, ALU.mult))
                v.wait_ge(act_b, 9)
                link(v.tensor_tensor(m4[:], m4[:], over_i(lns, whole), ALU.subtract), "col_ln")
                shape = [P, PAIRS, NS, NS]
                link(v.tensor_tensor(g_tok[:, :, :, 0:NS], gates[:, :, 0, :].unsqueeze(3).broadcast_to(shape),
                                     gates[:, :, 1, :].unsqueeze(2).broadcast_to(shape), ALU.mult))
                link(v.tensor_copy(g_tok[:, :, :, NS], mean.unsqueeze(2).broadcast_to([P, PAIRS, NS])), "g")
                v.wait_ge(act_b, 10)

                def sum_rows(k):
                    v.tensor_reduce(sums[:, streams[k]], m4[:, streams[k]], AX.X, ALU.add).then_inc(red[k], 1)

                def sum_cols(k):
                    v.tensor_reduce(sums[:, streams[k]], cols(m4, streams[k]), AX.X, ALU.add).then_inc(red[k], 1)

                def scale(k, n, over):
                    g = streams[k]
                    v.wait_ge(rec[k], n + 1)
                    v.tensor_tensor(m4[:, g], m4[:, g], over(recs, g), ALU.mult).then_inc(mul[k], 1)

                for k in range(STREAMS):
                    sum_rows(k)
                with v.Fori(0, (ITERS - 1) // UNROLL) as i:
                    for it in range(UNROLL):
                        for half, over, sum_other in ((0, over_j, sum_cols), (1, over_i, sum_rows)):
                            n = i * (2 * UNROLL) + (it * 2 + half)
                            scale(0, n, over)
                            scale(1, n, over)
                            v.wait_ge(mul[0], n + 1)
                            sum_other(0)
                            v.wait_ge(mul[1], n + 1)
                            sum_other(1)
                            scale(2, n, over)
                            v.wait_ge(mul[2], n + 1)
                            sum_other(2)

                v.wait_ge(mul[STREAMS - 1], HALVES)
                done = [VB["g"]]

                def last(ins):
                    done[0] += 1
                    ins.then_inc(vec_b, 1)
                    v.wait_ge(vec_b, done[0])

                last(v.tensor_scalar(h_tok[:], cols(m4, whole), 1.0 / LIFT, gains[:, 4:5], ALU.mult, ALU.mult))
                dg = h_tok[:].rearrange("p a j k -> p a (j k)")[:, :, 0:NS * NS:NS + 1]
                last(v.tensor_tensor(dg, dg, diag.unsqueeze(2).broadcast_to([P, PAIRS, NS]), ALU.add))
                assert done[0] == VB["h"]
                v.wait_ge(h_row_rdy, 1)
                v.wait_ge(gz_mm, PAIRS)

                def rows_out(s):
                    v.wait_ge(hx_mm, s.p + 1)
                    if s.fixed and s.p < KEPT:
                        v.tensor_tensor(tiles(row(z_all, s)), tiles(m_ps[s.c % 4]), of_pair(g_row, s, slice(NS, NG1))
                                        .broadcast_to([P, QT, DIM]), ALU.add).then_inc(out_rdy, 1)
                    else:
                        v.wait_ge(y_rdy, s.p - (KEPT - 1))
                        v.tensor_tensor(row(z_all, s), m_ps[s.c % 4], row(z_all, s), ALU.add).then_inc(out_rdy, 1)

                def mix_pair(s):
                    if s.b == 0:
                        if s.at(-4).exists():
                            v.wait_ge(hx_mm, s.p - 3)
                        v.tensor_tensor(h_bd[s.c % 4][:], tok_mask, own_token(h_row, s), ALU.mult).then_inc(h_rdy[0], 1)
                    if s.at(-3).exists():
                        rows_out(s.at(-3))

                run_mix(v, mix_pair, 4, 2)
                for c in range(1, 4):
                    rows_out(Step(PAIRS // 4 - 1, c, 4))

            @block.scalar
            def _(a):
                a.wait_ge(small_ld, 16)
                a.activation(gains[:, 0:1], small_sb[:, C_GX:C_GX + 1], ACT.Tanh).then_inc(act_g, 1)
                a.activation(gains[:, 1:2], small_sb[:, C_GF:C_GF + 1], ACT.Tanh).then_inc(act_g, 1)
                a.preload_act_table_set("natural_log_exp_and_others")
                a.activation(gains[:, 2:3], small_sb[:, C_GATE:C_GATE + 1], ACT.Exp, scale=-1.0).then_inc(act_g, 1)

                def pair(s):
                    s2, s1, m2, m3 = s.at(2), s.at(1), s.at(-2), s.at(-3)
                    for g in range(NG):
                        n = Group(s, g)
                        if g == 2 and m3.exists():
                            a.wait_ge(z_mm, m3.p + 1)
                            a.copy(row(z_all, m3), a_ps[:]).then_inc(z_ev, 1)
                        if g == 2 and s1.exists():
                            a.wait_ge(k_mm, s1.p + 1)
                            if s1.fixed and s1.p == 0:
                                a.wait_ge(gain_rdy, 3)
                                a.wait_ge(const_ld, 16)
                            for h in range(V):
                                ins = a.activation(k_bd[s1.b][:, h, PAD:PAD + T], b_ps[:], ACT.Identity,
                                                   scale=head_mask[:, h:h + 1], bias=bk_head[:, h:h + 1])
                            ins.then_inc(k_ev, 1)
                        if g == 3 and s1.exists():
                            a.wait_ge(v_mm, s1.p + 1)
                            if s1.at(-2).exists():
                                a.wait_ge(vt, s1.p - 1)
                            a.activation(v_sb[s1.b][:, PAD:PAD + T], a_ps[:], ACT.Identity,
                                         bias=small_sb[:, C_BV:C_BV + 1]).then_inc(v_ev, 1)
                        if g == 3 and s2.exists():
                            a.wait_ge(st1, s2.p + 1)
                            if s.exists():
                                a.wait_ge(xn_rdy, s.p + 1)
                            a.activation(ln1[s2.b][:, 0:1], mv1[s2.b][:, 1:2], ACT.Ln, bias=LN_EPS).then_inc(ln1_a, 1)
                            a.wait_ge(ln1_a, s2.p + 1)
                            a.activation(ln1[s2.b][:, 1:2], ln1[s2.b][:, 0:1], ACT.Exp, scale=-0.5).then_inc(y1, 1)
                        if g == 3 and m2.exists():
                            a.wait_ge(xt_mm, m2.p + 1)
                            if m2.at(-2).exists():
                                a.wait_ge(z_mm, m2.p - 1)
                            a.copy(xr_t[m2.b][:].rearrange("p (k j) -> p j k", j=NS),
                                   a_ps[:].rearrange("p (j k) -> p j k", j=NS)).then_inc(xt_ev, 1)
                        if g == 3 and s.fixed and s.p == PAIRS + 1:
                            after("w")
                            ln_exp(tok[:, 7, :], 0.0)
                        if g == 2 and s.fixed and s.p == PAIRS + 1:
                            a.wait_ge(mvc, PAIRS)
                            ln_exp(mv_all[:, :, 1], LN_EPS)
                        if n.exists():
                            a.wait_ge(sub, n.n + 1)
                            a.activation(prob[n.b][:, :, 0:KW], prob[n.b][:, :, 0:KW], ACT.Exp, scale=SCALE).then_inc(ex, 1)
                        draining = s.fixed and s.p >= PAIRS
                        if g == 1 and m3.exists() and not draining:
                            a.wait_ge(l_mm, m3.p + 1)
                            a.wait_ge(pv, n.n - 1)
                            a.copy(row(logit, m3), l_ps).then_inc(l_ev, 1)
                        if n.at(-2).exists():
                            m = n.at(-2)
                            a.wait_ge(pv, m.n + 1)
                            if m.at(-2).exists():
                                a.wait_ge(rd, m.n - 1)
                            o_all = o_ps[:, :, 0:U * VW].rearrange("p e (u w) -> p e u w", w=VW)
                            a.copy(den[m.b][:], o_all[:, :, :, TB]).then_inc(dn, 1)
                            if m.g == 0 and m.step.at(-2).exists():
                                a.wait_ge(oc, m.step.p - 1)
                            for h in range(V):
                                r = slice(TB * h, TB * h + TB)
                                dst = o_t[m.step.b][r, m.g * GT * U:(m.g + 1) * GT * U, :]
                                ins = a.copy(dst.rearrange("p (e u) d -> p e u d", u=U),
                                             o_all[r, :, :, h * HD:(h + 1) * HD])
                            ins.then_inc(ov, 1)
                        if g == 1 and m3.exists() and draining:
                            a.wait_ge(l_mm, m3.p + 1)
                            a.copy(row(logit, m3), l_ps).then_inc(l_ev, 1)
                        if n.exists() and n.at(2).exists():
                            a.copy(s_ps[n.b][:, :, 0:2 * V * KW].rearrange("p h (a k) -> p h a k", k=KW),
                                   consts_sb[:, K_MASK:K_MASK + KW].unsqueeze(1).unsqueeze(1)
                                   .broadcast_to([P, 2, 2 * V, KW])).then_inc(mk, 1)
                        if g == 0 and s1.exists():
                            a.wait_ge(q_mm, s1.p + 1)
                            if s1.fixed and s1.p < 2:
                                a.wait_ge(cleared if s1.p else zeroed, 3 if s1.p else NZERO)
                            if s1.at(-2).exists():
                                a.wait_ge(sc, s1.at(-1).p * NG)
                            for u in range(U):
                                r = slice(TB * u, TB * u + TB)
                                ins = a.activation(q_bd[s1.b][r, :, u, :],
                                                   a_ps[r, :].rearrange("p (a t) -> p a t", t=TB),
                                                   ACT.Identity, bias=small_sb[r, C_BQ:C_BQ + 1])
                            ins.then_inc(q_ev, 1)
                        if g == 0 and m2.exists():
                            a.wait_ge(st2, m2.p + 1)
                            if m2.at(-2).exists():
                                a.wait_ge(xn2_rdy, m2.p - 1)
                            a.activation(ln2[m2.b][:, 0:1], mv2[m2.b][:, 1:2], ACT.Ln, bias=LN_EPS).then_inc(ln2_a, 1)
                            a.wait_ge(ln2_a, m2.p + 1)
                            a.activation(ln2[m2.b][:, 1:2], ln2[m2.b][:, 0:1], ACT.Exp, scale=-0.5).then_inc(y2, 1)

                done = [0]

                def answer(ins):
                    done[0] += 1
                    ins.then_inc(act_b, 1)
                    return done[0]

                def after(name):
                    a.wait_ge(vec_b, VB[name])

                def ln_exp(src, bias):
                    a.wait_ge(act_b, answer(a.activation(tok[:, 0, :], src, ACT.Ln, bias=bias)))
                    answer(a.activation(tok[:, 1, :], tok[:, 0, :], ACT.Exp, scale=-0.5))

                run_pairs(a, pair)
                after("z_sub")
                answer(a.activation(e4[:], m4[:], ACT.Exp, scale=1.0 / TAU))
                after("gates_sub")
                answer(a.activation(gates[:], gates[:], ACT.Exp))
                after("row_sum")
                answer(a.activation(lns[:], sums[:], ACT.Ln))
                after("col_sub")
                answer(a.activation(e4[:], m4[:], ACT.Exp))
                after("col_sum")
                answer(a.activation(lns[:], sums[:], ACT.Ln))
                after("col_ln")
                answer(a.activation(m4[:], m4[:], ACT.Exp, bias=LN_LIFT))

                def logs(k, n):
                    g = streams[k]
                    a.wait_ge(red[k], n + 1)
                    a.activation(lns[:, g], sums[:, g], ACT.Ln, scale=1.0 / LIFT).then_inc(lnd[k], 1)

                def reciprocals(k, n):
                    g = streams[k]
                    a.wait_ge(lnd[k], n + 1)
                    a.activation(recs[:, g], lns[:, g], ACT.Exp, scale=-1.0).then_inc(rec[k], 1)

                def iteration(it):
                    for half in range(2):
                        n = it * 2 + half
                        logs(0, n)
                        logs(1, n)
                        reciprocals(0, n)
                        reciprocals(1, n)
                        logs(2, n)
                        reciprocals(2, n)

                def copy_branch(s):
                    a.wait_ge(gz_mm, s.p - (KEPT - 1))
                    a.copy(row(z_all, s), m_ps[s.b]).then_inc(gz_ev, 1)

                def seven(i, copies=False):
                    for it in range(UNROLL):
                        iteration(i * UNROLL + it)
                        if copies and it % 2 == 0:
                            copy_branch(Step(i, it // 2 + KEPT - 8, 4))

                seven(0)
                a.wait_ge(g_mv, 1)
                a.copy(flat(g_row), a_ps[:, 0:QT * PAIRS * NG1]).then_inc(g_row_rdy, 1)
                seven(1)
                with a.Fori(2, 2 + (PAIRS - KEPT) // 4) as i:
                    seven(i, copies=True)
                for i in range(2 + (PAIRS - KEPT) // 4, (ITERS - 1) // UNROLL):
                    seven(i)
                a.wait_ge(h_mv, 1)
                a.copy(flat(h_row), b_ps[:, 0:QT * PAIRS * NS]).then_inc(h_row_rdy, 1)

            @block.gpsimd
            def _(pool):
                pool.memset(q_bd[0][:], 0.0).then_inc(zeroed, 1)

                def pair(s):
                    s2, m1, m2 = s.at(2), s.at(-1), s.at(-2)
                    for g in range(NG):
                        n = Group(s, g)
                        if g == 0 and m2.exists():
                            pool.wait_ge(st2, m2.p + 1)
                            settle(pool)
                            pool.tensor_copy(row(mv_all, m2), mv2[m2.b][:]).then_inc(mvc, 1)
                        if g == 3 and s2.exists() and not (s2.fixed and s2.p == 0):
                            normalise_input(pool, s2)
                        if n.at(-3).exists():
                            m = n.at(-3)
                            pool.wait_ge(ov, m.n + 1)
                            pool.wait_ge(rd, m.n + 1)
                            o = o_t[m.step.b][:, m.g * GT * U:(m.g + 1) * GT * U, :]
                            pool.tensor_tensor(o, o, rden[m.b][:].rearrange("p e u -> p (e u)").unsqueeze(2)
                                               .broadcast_to([P, GT * U, HD]), ALU.mult).then_inc(nrm, 1)
                        if g == 0 and m1.exists():
                            if m1.fixed and m1.p == 0:
                                pool.wait_ge(gain_rdy, 3)
                            pool.wait_ge(r_ld[m1.b], m1.uses * 16)
                            settle(pool)
                            pool.tensor_scalar(x_res[m1.b][:], x_res[m1.b][:], gains[:, 3:4], None,
                                               ALU.add).then_inc(xres, 1)

                run_pairs(pool, pair)

                def spread_branch(dst, s):
                    pool.tensor_tensor(dst[:], tok_mask, own_token(g_row, s), ALU.mult).then_inc(g_rdy, 1)

                def branch_coefficients(s):
                    if s.fixed and s.p < KEPT + 2:
                        spread_branch(gbd[s.b], s)
                    else:
                        pool.wait_ge(gz_mm, s.p - (KEPT + 1))
                        spread_branch(gbd[s.b], s)
                        add_mean(s.at(-2))

                def add_mean(s):
                    pool.wait_ge(gz_ev, s.p - (KEPT - 1))
                    y = tiles(row(z_all, s))
                    pool.tensor_tensor(y, y, of_pair(g_row, s, slice(NS, NG1)).broadcast_to([P, QT, DIM]),
                                       ALU.add).then_inc(y_rdy, 1)

                pool.wait_ge(g_row_rdy, 1)
                run_branch(pool, branch_coefficients)
                for c in range(2):
                    add_mean(Step(PAIRS // 2 - 1, c))
                pool.wait_ge(gz_mm, PAIRS - KEPT)
                for c in range(KEPT):
                    spread_branch(h_bd[c], Step(0, c, KEPT))

                pool.wait_ge(h_row_rdy, 1)
                pool.wait_ge(gz_mm, PAIRS)

                def row_coefficients(s):
                    if s.b == 1:
                        if s.at(-4).exists():
                            pool.wait_ge(hx_mm, s.p - 3)
                        pool.tensor_tensor(h_bd[s.c % 4][:], tok_mask, own_token(h_row, s), ALU.mult)\
                            .then_inc(h_rdy[1], 1)

                run_mix(pool, row_coefficients, 4)


VB = {"w": 10, "z_sub": 18, "gates_sub": 20, "row_sum": 21, "col_sub": 24, "col_sum": 27, "col_ln": 30, "g": 32, "h": 34}


def kernel(**inputs):
    import concourse.bacc as bacc
    from concourse.bass_utils import run_bass_kernel_spmd

    a = {k: np.asarray(val) for k, val in inputs.items()}
    f32 = np.float32

    small = np.zeros((P, NSMALL), f32)
    for col, name in ((C_BQ, "bq"), (C_BK, "bk"), (C_BV, "bv"), (C_BO, "bo")):
        for b in range(2):
            small[b * C:(b + 1) * C, col] = a["L0_xattn_" + name]
    small[:, C_GX], small[:, C_GF], small[:, C_GATE] = a["g_xattn"][0], a["g_ffn"][0], a["L0_ffn_gate"][0]
    small[:, C_BASE:C_BASE + NS * NS] = a["L0_ffn_H_res_base"].reshape(1, -1)
    small[:, C_BASE + NS * NS:C_BASE + NS * NS + NS] = a["L0_ffn_H_pre_base"][None]
    small[:, C_BASE + NS * NS + NS:] = a["L0_ffn_H_post_base"][None]

    consts = np.zeros((P, NCONST), f32)
    for p in range(P):
        consts[p, K_ID + p] = 1.0
        t = p % TB
        consts[p, K_MASK:K_MASK + KW] = NEG
        consts[p, K_MASK + t:K_MASK + t + WINDOW] = 0.0
        consts[p, K_HEAD + (p // HD) % V] = 1.0
        consts[p, K_TOK + (p // NS) * NS:K_TOK + (p // NS) * NS + NS] = 1.0

    w4 = np.zeros((P, 4, P), f32)
    for b in range(2):
        r = slice(b * C, (b + 1) * C)
        for k, name in enumerate(("Wq", "Wk", "Wv")):
            w4[r, k, r] = a["L0_xattn_" + name].T
        for h in range(HEADS):
            to = (h % V) * U * HD + (b * (HEADS // V) + h // V) * HD
            w4[to:to + HD, 3, r] = a["L0_xattn_Wo"].T[h * HD:(h + 1) * HD]

    wl = np.concatenate([a["L0_ffn_W_res"], a["L0_ffn_W_pre"], a["L0_ffn_W_post"]])
    wl = np.ascontiguousarray(wl.reshape(NLOG, NS, DIM).transpose(2, 1, 0))

    pick_rows = np.zeros((P, NPICK), f32)
    pick_rows[np.arange(P), NS * np.arange(P) + NS - 1] = 1.0

    arrays = {"x": a["x"], "ctx": a["ctx_4096"], "small": small, "consts": consts, "pick": pick_rows, "w4": w4, "wl": wl,
              "wb": a["L0_ffn_W_branch"]}
    nc = bacc.Bacc("TRN2", target_bir_lowering=False, num_devices=1)
    aps = [nc.dram_tensor(k, val.shape, F32, kind="ExternalInput").ap() for k, val in arrays.items()]
    out = nc.dram_tensor("out", (B, C, T), F32, kind="ExternalOutput").ap()
    xn_dram = nc.dram_tensor("xn_scratch", (NTOK, T), F32, kind="Internal").ap()
    build(nc, *aps, out, xn_dram)
    r = run_bass_kernel_spmd(nc, [{k: np.ascontiguousarray(val) for k, val in arrays.items()}], core_ids=[0])
    return r.results[0]["out"]
```
